# Optimizing a Trainium2 kernel written in Bass

```python
import numpy as np
import jax
import jax.numpy as jnp

def _softmax(x, axis=-1):
    return jax.nn.softmax(x, axis=axis)

def _gelu(x):
    return jax.nn.gelu(x, approximate=True)

def _silu(x):
    return jax.nn.silu(x)

def _sigmoid(x):
    return jax.nn.sigmoid(x)

def _layernorm(x, axis=-1, eps=1e-05):
    m = jnp.mean(x, axis=axis, keepdims=True)
    v = jnp.var(x, axis=axis, keepdims=True)
    return (x - m) / jnp.sqrt(v + eps)

def _scatter_add(tgt, idx, src, axis=0):
    return tgt.at[idx].add(src)

def _segment_sum(src, seg, n):
    return jax.ops.segment_sum(src, seg, n)
kernel_name = 'mk_prb_d1_jaxref_r4_c99b77'

def setup_inputs(seed: int=0):
    np.random.seed(seed)
    _w = jnp.asarray

    def _L0_attn_setup():
        import jax, jax.numpy as jnp
        import numpy as np
        HIDDEN = 256
        HEADS = 16
        HEAD_DIM = HIDDEN // HEADS
        SCALE = HEAD_DIM ** (-0.5)
        key = jax.random.key(seed)
        ks = jax.random.split(key, 9)
        init = 1.0 / np.sqrt(HIDDEN)
        hidden_states = jax.random.normal(ks[0], (8, 256, HIDDEN), dtype=jnp.float32)

        def lin(k):
            kw, kb = jax.random.split(k)
            W = jax.random.uniform(kw, (HIDDEN, HIDDEN), jnp.float32, -init, init)
            b = jax.random.uniform(kb, (HIDDEN,), jnp.float32, -init, init)
            return (W, b)
        Wq, bq = lin(ks[1])
        Wk, bk = lin(ks[2])
        Wv, bv = lin(ks[3])
        Wo, bo = lin(ks[4])
        return {'hidden_states': hidden_states, 'Wq': Wq, 'bq': bq, 'Wk': Wk, 'bk': bk, 'Wv': Wv, 'bv': bv, 'Wo': Wo, 'bo': bo}
    _L0_attn_in = _L0_attn_setup()

    def _L0_ffn_setup():
        import jax, jax.numpy as jnp
        import numpy as np
        N_EXPERTS = 16
        TOPK = 2
        CAPACITY_FACTOR = 1.0
        EPS_GATE = 1e-06
        LN_EPS = 1e-05
        key = jax.random.key(seed)
        ks = jax.random.split(key, 8)
        B, S, D, F, E = (4, 512, 256, 1024, N_EXPERTS)
        Fp = F // E
        s = 0.02
        return {'x': jax.random.normal(ks[0], (B, S, D), dtype=jnp.float32), 'wg': s * jax.random.normal(ks[1], (D, E), dtype=jnp.float32), 'bg': jnp.zeros((E,), dtype=jnp.float32), 'w1': s * jax.random.normal(ks[2], (E, D, Fp), dtype=jnp.float32), 'b1': jnp.zeros((E, Fp), dtype=jnp.float32), 'w2': s * jax.random.normal(ks[3], (E, Fp, D), dtype=jnp.float32), 'b2': jnp.zeros((E, D), dtype=jnp.float32), 'gamma': jnp.ones((D,), dtype=jnp.float32), 'beta': jnp.zeros((D,), dtype=jnp.float32)}
    _L0_ffn_in = _L0_ffn_setup()
    _d = {'L0_attn_hidden_states': _L0_attn_in['hidden_states'], 'L0_attn_Wq': _L0_attn_in['Wq'], 'L0_attn_bq': _L0_attn_in['bq'], 'L0_attn_Wk': _L0_attn_in['Wk'], 'L0_attn_bk': _L0_attn_in['bk'], 'L0_attn_Wv': _L0_attn_in['Wv'], 'L0_attn_bv': _L0_attn_in['bv'], 'L0_attn_Wo': _L0_attn_in['Wo'], 'L0_attn_bo': _L0_attn_in['bo'], 'L0_ffn_wg': _L0_ffn_in['wg'], 'L0_ffn_bg': _L0_ffn_in['bg'], 'L0_ffn_w1': _L0_ffn_in['w1'], 'L0_ffn_b1': _L0_ffn_in['b1'], 'L0_ffn_w2': _L0_ffn_in['w2'], 'L0_ffn_b2': _L0_ffn_in['b2'], 'L0_ffn_gamma': _L0_ffn_in['gamma'], 'L0_ffn_beta': _L0_ffn_in['beta']}
    _x0 = _d['L0_attn_hidden_states']
    _d['L0_attn_hidden_states'] = jax.random.normal(jax.random.fold_in(jax.random.key(seed), 1), (4, 2048, 256), dtype=_x0.dtype)
    del _x0
    return _d

def reference(L0_attn_hidden_states, L0_attn_Wq, L0_attn_bq, L0_attn_Wk, L0_attn_bk, L0_attn_Wv, L0_attn_bv, L0_attn_Wo, L0_attn_bo, L0_ffn_wg, L0_ffn_bg, L0_ffn_w1, L0_ffn_b1, L0_ffn_w2, L0_ffn_b2, L0_ffn_gamma, L0_ffn_beta):

    def _L0_attn_ref(hidden_states, Wq, bq, Wk, bk, Wv, bv, Wo, bo):
        import jax, jax.numpy as jnp
        import numpy as np
        HIDDEN = 256
        HEADS = 16
        HEAD_DIM = HIDDEN // HEADS
        SCALE = HEAD_DIM ** (-0.5)
        b, s, d = hidden_states.shape
        q = (hidden_states @ Wq.T + bq).reshape(b, s, HEADS, HEAD_DIM)
        k = (hidden_states @ Wk.T + bk).reshape(b, s, HEADS, HEAD_DIM)
        v = (hidden_states @ Wv.T + bv).reshape(b, s, HEADS, HEAD_DIM)
        q = q * SCALE
        scores = jnp.einsum('bqhd,bkhd->bhqk', q, k)
        probs = jax.nn.softmax(scores.astype(jnp.float32), axis=-1).astype(scores.dtype)
        out = jnp.einsum('bhqk,bkhd->bqhd', probs, v).reshape(b, s, d)
        return out @ Wo.T + bo

    def _L0_ffn_ref(x, wg, bg, w1, b1, w2, b2, gamma, beta):
        import jax, jax.numpy as jnp
        import numpy as np
        N_EXPERTS = 16
        TOPK = 2
        CAPACITY_FACTOR = 1.0
        EPS_GATE = 1e-06
        LN_EPS = 1e-05
        B, S, D = x.shape
        E = wg.shape[1]
        capacity = int(CAPACITY_FACTOR * B)
        scores = jax.nn.softmax(x @ wg + bg, axis=-1)
        _, top_i = jax.lax.top_k(scores, TOPK)
        mask = jax.nn.one_hot(top_i, E, dtype=scores.dtype).sum(-2)
        masked = scores * mask
        denom = masked.sum(0, keepdims=True) + EPS_GATE
        route = masked / denom * capacity
        route_e = jnp.transpose(route, (2, 0, 1))
        max_len = S // 2
        _, seq_ids = jax.lax.top_k(route_e, max_len)
        seq_ids = jnp.sort(seq_ids, axis=-1)
        b_idx = jnp.arange(B)[None, :, None]
        xg = x[b_idx, seq_ids]
        h = jnp.einsum('ebld,edf->eblf', xg, w1) + b1[:, None, None, :]
        h = jax.nn.gelu(h, approximate=False)
        out = jnp.einsum('eblf,efd->ebld', h, w2) + b2[:, None, None, :]
        outs = jnp.zeros_like(x).at[b_idx, seq_ids].add(out)
        z = x + outs
        mu = z.mean(-1, keepdims=True)
        var = ((z - mu) ** 2).mean(-1, keepdims=True)
        return (z - mu) / jnp.sqrt(var + LN_EPS) * gamma + beta
    x = L0_attn_hidden_states
    xn = _layernorm(x, axis=-1)
    x = x + _L0_attn_ref(xn, L0_attn_Wq, L0_attn_bq, L0_attn_Wk, L0_attn_bk, L0_attn_Wv, L0_attn_bv, L0_attn_Wo, L0_attn_bo) + _L0_ffn_ref(xn, L0_ffn_wg, L0_ffn_bg, L0_ffn_w1, L0_ffn_b1, L0_ffn_w2, L0_ffn_b2, L0_ffn_gamma, L0_ffn_beta)
    return x

_drawn_inputs = setup_inputs


def setup_inputs(seed=0):
    import zlib

    import numpy as np

    out = dict(_drawn_inputs(seed))
    spreads = {'L0_ffn_bg': (0.0, 0.757),
     'L0_ffn_b1': (0.0, 2.0),
     'L0_ffn_b2': (0.0, 0.321),
     'L0_ffn_gamma': (1.0, 0.6),
     'L0_ffn_beta': (0.0, 0.8)}
    factors = {'L0_attn_Wq': 8.0,
     'L0_attn_bq': 8.0,
     'L0_attn_Wk': 8.0,
     'L0_attn_bk': 64.0,
     'L0_attn_Wv': 8.0,
     'L0_attn_bv': 5.15,
     'L0_attn_Wo': 4.423,
     'L0_attn_bo': 17.111,
     'L0_ffn_wg': 4.862,
     'L0_ffn_w1': 7.169,
     'L0_ffn_w2': 3.164}
    for name, (base, spread) in spreads.items():
        noise = np.random.default_rng([zlib.crc32(name.encode()), seed]).standard_normal(out[name].shape)
        drawn = base * np.exp(spread * noise) if base else spread * noise
        out[name] = jnp.asarray(drawn.astype(out[name].dtype))
    for name, factor in factors.items():
        out[name] = (out[name] * factor).astype(out[name].dtype)
    return out
```

```python
from contextlib import ExitStack

import concourse.bass as bass
from concourse import mybir
from concourse.alu_op_type import AluOpType as ALU

F32 = mybir.dt.float32
BF16 = mybir.dt.bfloat16
I32 = mybir.dt.int32
ACT = mybir.ActivationFunctionType
AX = mybir.AxisListType
ds = bass.ds

P = 128
B, S, D = 4, 2048, 256
H = 16
HD = D // H
E, F = 16, 64
TOPK_TOKENS = S // 2
TOKENS = B * S
TILES = TOKENS // P
BLK = 512
TPB = BLK // P
NBLK = TOKENS // BLK
BPS = S // BLK
ST = S // P
KC = D // P
EP = E // 2
HEADS = B * H
EPS_LN, EPS_GATE = 1e-5, 1e-6
SCALE = float(HD) ** -0.5
PARTS = 3
Q_ORDER = [(0, 3), (1, 2), (2, 1)]
K_ORDER = [(0, 3), (0, 2), (0, 1)]
FEAT = 6 * HD
SHIFT = PARTS
VW = 32


class Chain:

    def __init__(self, eng, sem, base=0):
        self.eng, self.sem, self.base, self.n = eng, sem, base, 0

    def __call__(self, ins):
        self.n += 1
        ins.then_inc(self.sem, 1)
        self.eng.wait_ge(self.sem, self.base + self.n)


def wait_apart(eng, sem, value, passed):
    eng.wait_ge(sem, value)
    eng.sem_inc(passed, 1)


def build(nc, x, wqT, wkT, wvT, woT, bq, bk, bv, bo, wg, bg, w1, b1, w2, b2, gamma, beta, out):
    top = ExitStack()
    with top:
        def sb(name, shape, dt=F32, ctx=top):
            return ctx.enter_context(nc.sbuf_tensor(name, shape, dt))

        def ps(name, shape, ctx):
            return ctx.enter_context(nc.psum_tensor(name, shape, F32))

        def sem(name):
            return top.enter_context(nc.semaphore(name))

        q_parts = nc.dram_tensor("q_parts", [PARTS, B * D, S], BF16).ap()
        k_parts = nc.dram_tensor("k_parts", [PARTS, B * D, S], BF16).ap()
        att_dram = nc.dram_tensor("att_dram", [HEADS, P, BLK], F32).ap()
        mask_f = nc.dram_tensor("mask_f", [B * E, S], F32).ap()
        mask_b = nc.dram_tensor("mask_b", [B * E, S], BF16).ap()

        passed = [sem(f"passed_{e}") for e in ("dve", "pe", "pool")]
        x_blocks = x.rearrange("(n t p) d -> n p t d", p=P, t=TPB)
        out_blocks = out.rearrange("(n t p) d -> n p t d", p=P, t=TPB)

        tok_all = sb("tok_all", [P, NBLK, KC * BLK])
        v_all = sb("v_all", [P, B, H, ST, HD])
        woT_sb = sb("woT_sb", [P, KC, D])
        ident = sb("ident", [P, P])

        setup_stage = ExitStack()
        early = setup_stage
        with early:
            w1_sb = sb("w1_sb", [P, KC, E * F], ctx=early)
            b2_sb = sb("b2_sb", [E, D], ctx=early)
            b1_col = sb("b1_col", [P, EP], ctx=early)
            gamma_bc = sb("gamma_bc", [P, D], ctx=early)
            shift_bc = sb("shift_bc", [P, D], ctx=early)
            stats_all = sb("stats_all", [P, TILES, 2], ctx=early)
            minus_half = sb("minus_half", [P, TPB], ctx=early)

            mid = ExitStack()
            with mid:
                wqT_sb = sb("wqT_sb", [P, KC, D], ctx=mid)
                wkT_sb = sb("wkT_sb", [P, KC, D], ctx=mid)
                wvT_sb = sb("wvT_sb", [P, KC, D], ctx=mid)
                wg_sb = sb("wg_sb", [P, KC, E], ctx=mid)
                bg_bc = sb("bg_bc", [P, E], ctx=mid)
                bv_bc = sb("bv_bc", [P, D], ctx=mid)
                bq_col = sb("bq_col", [P, KC], ctx=mid)
                bqs_col = sb("bqs_col", [P, KC], ctx=mid)
                bk_col = sb("bk_col", [P, KC], ctx=mid)
                logits = sb("logits", [P, TILES, E], ctx=mid)
                with ExitStack() as st:
                    bo_bc = sb("bo_bc", [P, D], ctx=st)
                    setup(nc, sem, locals())
                with ExitStack() as st:
                    norm(nc, sem, lambda *a: sb(*a, ctx=st), lambda *a: ps(*a, ctx=st), locals())
                with ExitStack() as st:
                    project(nc, sem, lambda *a: sb(*a, ctx=st), lambda *a: ps(*a, ctx=st), locals())
            with ExitStack() as st:
                experts(nc, sem, lambda *a: sb(*a, ctx=st), lambda *a: ps(*a, ctx=st), locals())
        with ExitStack() as st:
            attend(nc, sem, lambda *a: sb(*a, ctx=st), lambda *a: ps(*a, ctx=st), locals())
        with ExitStack() as st:
            output(nc, sem, lambda *a: sb(*a, ctx=st), lambda *a: ps(*a, ctx=st), locals())


def setup(nc, sem, t):
    loaded, made, base = sem("setup_loaded"), sem("setup_made"), sem("setup_sum")
    with nc.Block() as block:
        @block.sync
        def _(sp):
            loads = [(t[w + "_sb"][:, :, :], t[w].rearrange("(c p) n -> p c n", p=P))
                     for w in ("wqT", "wkT", "wvT", "woT", "wg", "w1")]
            loads.append((t["b2_sb"][:, :], t["b2"]))
            loads += [(t[c][:, :], t[a]) for c, a in (("b1_col", "b1"), ("bq_col", "bq"), ("bk_col", "bk"))]
            loads += [(t[c][:, :], t[a].partition_broadcast(P)) for c, a in
                      (("gamma_bc", "gamma"), ("shift_bc", "beta"), ("bo_bc", "bo"),
                       ("bg_bc", "bg"), ("bv_bc", "bv"))]
            for dst, src in loads:
                sp.dma_start(dst, src).then_inc(loaded, 16)
            sp.wait_ge(loaded, 16 * len(loads))
            sp.sem_inc(base, 1)

        @block.gpsimd
        def _(pool):
            pool.memset(t["ident"][:, :], 0.0).then_inc(made, 1)
            pool.memset(t["minus_half"][:, :], -0.5)
            pool.wait_ge(made, 1)
            pool.affine_select(out=t["ident"][:, :], in_=t["ident"][:, :], compare_op=ALU.not_equal,
                               fill=1.0, base=0, pattern=[[-1, P]], channel_multiplier=1)

        @block.vector
        def _(dve):
            dve.wait_ge(base, 1)
            dve.tensor_tensor(t["shift_bc"][:, :], t["shift_bc"][:, :], t["bo_bc"][:, :], ALU.add)
            dve.tensor_scalar(t["bqs_col"][:, :], t["bq_col"][:, :], SCALE, None, ALU.mult)


def norm(nc, sem, sb, ps, t):
    x_in = [sb(f"x_in{u}", [P, TPB, D]) for u in range(2)]
    xn = [sb(f"xn{u}", [P, TPB, D]) for u in range(2)]
    xT = [sb(f"xT{u}", [P, KC, BLK]) for u in range(2)]
    bn = [sb(f"bn{u}", [P, TPB, 6]) for u in range(2)]
    mv = [sb(f"mv{u}", [P, TPB, 2]) for u in range(2)]
    var = [sb(f"var{u}", [P, TPB]) for u in range(2)]
    rstd = [sb(f"rstd{u}", [P, TPB]) for u in range(2)]
    xT_ps = [ps(f"xT_ps{c}", [P, BLK]) for c in range(KC)]
    lg_ps = ps("lg_ps", [P, TPB, E])
    v_ps = [ps(f"v_ps{j}", [P, 2, D]) for j in range(2)]
    logits, v_all, tok_all, stats = t["logits"], t["v_all"], t["tok_all"], t["stats_all"]
    v_view = v_all[:, :, :, :, :].rearrange("p b h s d -> p b s h d")

    x_loaded = [sem(f"n_x_loaded{u}") for u in range(2)]
    bn_done, mv_done, rstd_done = sem("n_bn"), sem("n_mv"), sem("n_rstd")
    pool_chain = sem("n_pool")
    xn_done = sem("n_xn")
    transposed = sem("n_transposed")
    xT_copied = sem("n_xT")
    ps_freed = sem("n_ps_freed")
    logits_done, logits_read = sem("n_lg"), sem("n_lg_read")
    v_done = sem("n_v")
    v_read = sem("n_v_read")

    with nc.Block() as block:
        @block.sync
        def _(sp):
            with sp.Fori(0, NBLK // 2) as i:
                for u in range(2):
                    blk = i * 2 + u
                    sp.wait_ge(xn_done, blk + 1)
                    sp.dma_start(x_in[u][:, :, :], t["x_blocks"][ds(blk, 1)].rearrange("n p t d -> (n p) t d")).then_inc(x_loaded[u], 16)

        @block.vector
        def _(dve):
            dve.sem_inc(xn_done, 2)
            dve.sem_inc(logits_read, 1)
            dve.sem_inc(v_read, 2)

            def normalise(blk, i, u):
                dve.wait_ge(x_loaded[u], i * 16 + 16)
                for k in range(TPB):
                    ins = dve.bn_stats(bn[u][:, k, :], x_in[u][:, k, :])
                ins.then_inc(bn_done, 1)
                wait_apart(dve, bn_done, blk + 1, t["passed"][0])
                for k in range(TPB):
                    ins = dve.bn_aggr(mv[u][:, k, :], bn[u][:, k, :])
                ins.then_inc(mv_done, 1)
                dve.wait_ge(rstd_done, blk + 1)
                dve.wait_ge(transposed, blk * 2 + 1)
                for k in range(TPB):
                    ins = dve.tensor_scalar(xn[u][:, k, :], x_in[u][:, k, :], mv[u][:, k, 0:1],
                                            rstd[u][:, k:k + 1], ALU.subtract, ALU.mult)
                ins.then_inc(xn_done, 1)

            def evacuate(blk, u):
                dve.wait_ge(logits_done, blk + 1)
                dve.tensor_tensor(logits[:, ds(blk * TPB, TPB), :], lg_ps[:, :, :],
                                  t["bg_bc"][:, :].unsqueeze(1).broadcast_to([P, TPB, E]),
                                  ALU.add).then_inc(logits_read, 1)
                for j in range(2):
                    dve.wait_ge(v_done, blk * 2 + j + 5)
                    dve.tensor_tensor(
                        v_view[:, ds(blk // BPS, 1), ds((blk % BPS) * TPB + 2 * j, 2), :, :].rearrange("p b s h d -> p (b s) h d"),
                        v_ps[j][:, :, :].rearrange("p s (h d) -> p s h d", h=H),
                        t["bv_bc"][:, :].rearrange("p (h d) -> p h d", h=H).unsqueeze(1).broadcast_to([P, 2, H, HD]),
                        ALU.add).then_inc(v_read, 1)

            normalise(0, 0, 0)
            with dve.Fori(0, NBLK // 2 - 1) as i:
                normalise(i * 2 + 1, i, 1)
                evacuate(i * 2, 0)
                normalise(i * 2 + 2, i + 1, 0)
                evacuate(i * 2 + 1, 1)
            normalise(NBLK - 1, NBLK // 2 - 1, 1)
            evacuate(NBLK - 2, 0)
            evacuate(NBLK - 1, 1)

        @block.gpsimd
        def _(pool):
            with pool.Fori(0, NBLK // 2) as i:
                for u in range(2):
                    blk = i * 2 + u
                    wait_apart(pool, mv_done, blk + 1, t["passed"][2])
                    pool.tensor_scalar(var[u][:, :], mv[u][:, :, 1], EPS_LN, None, ALU.add).then_inc(pool_chain, 1)
                    pool.tensor_copy(stats[:, ds(blk * TPB, TPB), 0], mv[u][:, :, 0])
                    pool.wait_ge(pool_chain, blk + 1)
                    pool.tensor_tensor(rstd[u][:, :], var[u][:, :], t["minus_half"][:, :], ALU.pow).then_inc(rstd_done, 1)
                    pool.wait_ge(rstd_done, blk + 1)
                    pool.tensor_copy(stats[:, ds(blk * TPB, TPB), 1], rstd[u][:, :])

        @block.scalar
        def _(act):
            act.sem_inc(ps_freed, 2)
            with act.Fori(0, NBLK // 2) as i:
                for u in range(2):
                    blk = i * 2 + u
                    for c in range(KC):
                        act.wait_ge(transposed, blk * 2 + c + 3)
                        if c == 0:
                            act.wait_ge(v_done, blk * 2 + 1)
                        act.activation(xT[u][:, c, :], xT_ps[c][:, :], ACT.Copy).then_inc(xT_copied, 1)
                        act.activation(tok_all[:, ds(blk, 1), c * BLK:(c + 1) * BLK].rearrange("p n s -> p (n s)"),
                                       xT_ps[c][:, :], ACT.Copy).then_inc(ps_freed, 1)

        @block.tensor
        def _(pe):
            pe.sem_inc(transposed, 2)
            pe.sem_inc(v_done, 4)

            def transpose(blk, u):
                pe.wait_ge(xn_done, blk + 3)
                for c in range(KC):
                    pe.wait_ge(ps_freed, blk * 2 + c + 1)
                    for k in range(TPB):
                        ins = pe.transpose(xT_ps[c][:, k * P:(k + 1) * P], xn[u][:, k, c * P:(c + 1) * P], t["ident"][:, :])
                    ins.then_inc(transposed, 1)

            def project_tokens(blk, u):
                pe.wait_ge(xT_copied, blk * 2 + 2)
                pe.wait_ge(logits_read, blk + 1)
                for k in range(TPB):
                    for c in range(KC):
                        ins = pe.matmul(lg_ps[:, k, :], xT[u][:, c, k * P:(k + 1) * P], t["wg_sb"][:, c, :],
                                        start=(c == 0), stop=(c == KC - 1))
                ins.then_inc(logits_done, 1)
                for j in range(2):
                    pe.wait_ge(v_read, blk * 2 + j + 1)
                    for k in range(2):
                        for c in range(KC):
                            tok = (2 * j + k) * P
                            ins = pe.matmul(v_ps[j][:, k, :], xT[u][:, c, tok:tok + P], t["wvT_sb"][:, c, :],
                                            start=(c == 0), stop=(c == KC - 1))
                    ins.then_inc(v_done, 1)

            transpose(0, 0)
            with pe.Fori(0, NBLK // 2 - 1) as i:
                transpose(i * 2 + 1, 1)
                project_tokens(i * 2, 0)
                transpose(i * 2 + 2, 0)
                project_tokens(i * 2 + 1, 1)
            transpose(NBLK - 1, 1)
            project_tokens(NBLK - 2, 0)
            project_tokens(NBLK - 1, 1)


def project(nc, sem, sb, ps, t):
    M = 2 * KC
    f32s = [sb(f"f32s{m}", [P, BLK]) for m in range(M)]
    rest = [sb(f"rest{m}", [P, BLK]) for m in range(M)]
    parts = [sb(f"parts{m}", [P, PARTS, BLK], BF16) for m in range(M)]
    qk_ps = [ps(f"qk_ps{m}", [P, BLK]) for m in range(M)]
    route_ps = ps("route_ps", [B * E, S])
    weights = [t["wqT_sb"], t["wqT_sb"], t["wkT_sb"], t["wkT_sb"]]
    biases = [t["bqs_col"], t["bqs_col"], t["bk_col"], t["bk_col"]]
    scales = [SCALE, SCALE, 1.0, 1.0]
    targets = [t["q_parts"], t["q_parts"], t["k_parts"], t["k_parts"]]

    scored = sem("p_scored")
    first = sem("p_first")
    rest_done = sem("p_rest")
    second = sem("p_second")
    third = sem("p_third")
    stored = [sem(f"p_stored{m}") for m in range(M)]
    shifted, exped = sem("p_shifted"), sem("p_exped")
    routed, route_t = sem("p_routed"), sem("p_route_t")
    masked, mask_stored = sem("p_masked"), sem("p_mask_stored")
    chain = sem("p_chain")
    loop_chain = sem("p_loop_chain")

    lg = t["logits"]
    work = sb("work", [P, 4, TILES, E])
    ex, tmp, hot, hot2 = (work[:, k] for k in range(4))
    red = sb("red", [P, TILES])
    order_i = sb("order_i", [P, E], I32)
    order = sb("order", [P, E])
    denom = sb("denom", [P, ST, E])
    gt = sb("gt", [B * E, S])
    junk = gt[:, 0:S // 2].bitcast(BF16)
    eq, cum = (work[0:B * E, 2 * k:2 * k + 2].rearrange("p k n e -> p (k n e)") for k in range(2))
    mask16 = cum[:, 0:S // 2].bitcast(BF16)
    low = sb("low", [B * E, 1], I32)
    bit = sb("bit", [B * E, 1], I32)
    cand = sb("cand", [B * E, 1], I32)
    take = sb("take", [B * E, 1], I32)
    count = sb("count", [B * E, 1])
    need = sb("need", [B * E, 1])
    ordered = sem("p_ordered")

    with nc.Block() as block:
        @block.tensor
        def _(pe):
            def chunks(lo, hi):
                with pe.Fori(lo, hi) as blk:
                    for m in range(M):
                        pe.wait_ge(first, blk * M + m + 1)
                        for c in range(KC):
                            half = m % KC
                            ins = pe.matmul(qk_ps[m][:, :], weights[m][:, c, half * P:(half + 1) * P],
                                            t["tok_all"][:, ds(blk, 1), c * BLK:(c + 1) * BLK].rearrange("p n s -> p (n s)"),
                                            start=(c == 0), stop=(c == KC - 1))
                        ins.then_inc(scored, 1)

            chunks(0, NBLK // 2)
            pe.wait_ge(routed, 1)
            for s in range(ST):
                ins = pe.transpose(route_ps[:, s * P:(s + 1) * P], tmp[:, s * B:(s + 1) * B, :].rearrange("p b e -> p (b e)"),
                                   t["ident"][:, :])
            ins.then_inc(route_t, 1)
            chunks(NBLK // 2, NBLK)

        @block.scalar
        def _(act):
            act.sem_inc(first, M)
            act.wait_ge(shifted, 1)
            act.activation(ex[:, :, :], lg[:, :, :], ACT.Exp).then_inc(exped, 1)

            def take_first(n, m, blk):
                act.wait_ge(scored, n + 1)
                act.wait_ge(rest_done, n + 1)
                act.activation(f32s[m][:, :], qk_ps[m][:, :], ACT.Identity, bias=biases[m][:, m % KC:m % KC + 1], scale=scales[m])
                act.wait_ge(stored[m], blk * 16 + 16)
                act.activation(parts[m][:, 0, :], qk_ps[m][:, :], ACT.Identity, bias=biases[m][:, m % KC:m % KC + 1],
                               scale=scales[m]).then_inc(first, 1)

            def take_second(n, m):
                act.wait_ge(rest_done, n + 1 + M)
                act.activation(parts[m][:, 1, :], rest[m][:, :], ACT.Copy).then_inc(second, 1)

            take_first(0, 0, 0)
            with act.Fori(0, NBLK - 1) as blk:
                for m in range(M):
                    take_first(blk * M + m + 1, (m + 1) % M, blk + (m + 1) // M)
                    take_second(blk * M + m, m)
            last = (NBLK - 1) * M
            for m in range(M):
                if m + 1 < M:
                    take_first(last + m + 1, m + 1, NBLK - 1)
                take_second(last + m, m)
            act.wait_ge(masked, 1)
            act.dma_start(t["mask_f"], gt[:, :]).then_inc(mask_stored, 16)
            act.dma_start(t["mask_b"], mask16).then_inc(mask_stored, 16)
            act.wait_ge(mask_stored, 32)

        @block.gpsimd
        def _(pool):
            pool.sem_inc(rest_done, M)
            pool.sem_inc(third, M)
            pool.iota(order_i[:, :], pattern=[[-1, E]], base=E, channel_multiplier=0).then_inc(ordered, 1)

            def take_rest(n, m):
                pool.wait_ge(first, n + 1 + M)
                pool.wait_ge(third, n + 1)
                pool.tensor_tensor(rest[m][:, :], f32s[m][:, :], parts[m][:, 0, :], ALU.subtract).then_inc(rest_done, 1)

            def take_third(n, m):
                pool.wait_ge(second, n + 1)
                pool.tensor_tensor(parts[m][:, 2, :], rest[m][:, :], parts[m][:, 1, :], ALU.subtract).then_inc(third, 1)

            take_rest(0, 0)
            with pool.Fori(0, NBLK - 1) as blk:
                for m in range(M):
                    take_rest(blk * M + m + 1, (m + 1) % M)
                    take_third(blk * M + m, m)
            last = (NBLK - 1) * M
            for m in range(M):
                if m + 1 < M:
                    take_rest(last + m + 1, m + 1)
                take_third(last + m, m)

        @block.sync
        def _(sp):
            for m in range(M):
                sp.sem_inc(stored[m], 16)
            with sp.Fori(0, NBLK) as blk:
                for m in range(M):
                    sp.wait_ge(third, blk * M + m + 1 + M)
                    row = (blk // BPS) * D + (m % KC) * P
                    sp.dma_start(targets[m][:, ds(row, P), ds((blk % BPS) * BLK, BLK)].rearrange("r p s -> p r s"),
                                 parts[m][:, :, :]).then_inc(stored[m], 16)
            for m in range(M):
                sp.wait_ge(stored[m], 16 * NBLK + 16)

        @block.vector
        def _(dve):
            do = Chain(dve, chain)
            wide = lambda a: a[:, :].unsqueeze(2).broadcast_to([P, TILES, E])
            do(dve.tensor_reduce(red[:, :], lg[:, :, :], AX.X, ALU.max))
            dve.tensor_tensor(lg[:, :, :], lg[:, :, :], wide(red), ALU.subtract).then_inc(shifted, 1)
            dve.wait_ge(exped, 1)
            do(dve.tensor_reduce(red[:, :], ex[:, :, :], AX.X, ALU.add))
            do(dve.reciprocal(red[:, :], red[:, :]))
            do(dve.tensor_tensor(ex[:, :, :], ex[:, :, :], wide(red), ALU.mult))
            dve.wait_ge(ordered, 1)
            do(dve.tensor_copy(order[:, :], order_i[:, :]))
            order_bc = order[:, :].unsqueeze(1).broadcast_to([P, TILES, E])
            scores = ex
            for k, h in enumerate((hot, hot2)):
                do(dve.tensor_reduce(red[:, :], scores[:, :, :], AX.X, ALU.max))
                do(dve.tensor_tensor(h[:, :, :], scores[:, :, :], wide(red), ALU.is_equal))
                do(dve.tensor_tensor(h[:, :, :], h[:, :, :], order_bc, ALU.mult))
                do(dve.tensor_reduce(red[:, :], h[:, :, :], AX.X, ALU.max))
                do(dve.tensor_tensor(h[:, :, :], h[:, :, :], wide(red), ALU.is_equal))
                if k == 0:
                    do(dve.scalar_tensor_tensor(tmp[:, :, :], hot[:, :, :], -4.0, ex[:, :, :], ALU.mult, ALU.add))
                    scores = tmp
            do(dve.tensor_tensor(hot[:, :, :], hot[:, :, :], hot2[:, :, :], ALU.add))
            do(dve.tensor_tensor(ex[:, :, :], ex[:, :, :], hot[:, :, :], ALU.mult))
            by_batch = ex[:, :, :].rearrange("p (b s) e -> p b s e", b=B)
            do(dve.tensor_tensor(denom[:, :, :], by_batch[:, 0], by_batch[:, 1], ALU.add))
            for b in range(2, B):
                do(dve.tensor_tensor(denom[:, :, :], denom[:, :, :], by_batch[:, b], ALU.add))
            do(dve.tensor_scalar(denom[:, :, :], denom[:, :, :], EPS_GATE, None, ALU.add))
            do(dve.reciprocal(denom[:, :, :], denom[:, :, :]))
            routes = tmp[:, :, :].rearrange("p (s b) e -> p b s e", b=B)
            for b in range(B):
                do(dve.scalar_tensor_tensor(routes[:, b], by_batch[:, b], float(B), denom[:, :, :], ALU.mult, ALU.mult))
            do(dve.memset(low[:, :], 0))
            dve.memset(bit[:, :], 1 << 30).then_inc(routed, 1)
            dve.wait_ge(route_t, 1)

            STEP = 6
            with dve.Fori(0, 31) as i:
                step = Chain(dve, loop_chain, i * STEP)
                step(dve.tensor_tensor(cand[:, :], low[:, :], bit[:, :], ALU.bitwise_or))
                step(dve.tensor_scalar(junk, route_ps[:, :], cand[:, :].bitcast(F32), None, ALU.is_ge, ALU.add,
                                       accum_out=count[:, :]))
                step(dve.tensor_scalar(take[:, :], count[:, :], TOPK_TOKENS - 0.5, -1.0, ALU.is_ge, ALU.mult))
                step(dve.tensor_tensor(take[:, :], take[:, :], bit[:, :], ALU.bitwise_and))
                step(dve.tensor_tensor(low[:, :], low[:, :], take[:, :], ALU.bitwise_or))
                step(dve.tensor_scalar(bit[:, :], bit[:, :], 1, None, ALU.logical_shift_right))
            bound = low[:, :].bitcast(F32)
            do(dve.tensor_scalar(gt[:, :], route_ps[:, :], bound, None, ALU.is_gt, ALU.add, accum_out=count[:, :]))
            do(dve.tensor_scalar(need[:, :], count[:, :], -1.0, float(TOPK_TOKENS), ALU.mult, ALU.add))
            do(dve.tensor_scalar(eq[:, :], route_ps[:, :], bound, None, ALU.is_equal))
            do(dve.tensor_tensor_scan(cum[:, :], eq[:, :], eq[:, :], 0.0, ALU.add, ALU.max))
            do(dve.scalar_tensor_tensor(eq[:, :], cum[:, :], need[:, :], eq[:, :], ALU.is_le, ALU.mult))
            do(dve.tensor_tensor(gt[:, :], gt[:, :], eq[:, :], ALU.add))
            dve.tensor_copy(mask16, gt[:, :]).then_inc(masked, 1)


def experts(nc, sem, sb, ps, t):
    w2_sb = sb("w2_sb", [P, EP, D])
    w2_loaded = sem("e_w2_loaded")
    mask_bc = [sb(f"mask_bc{u}", [P, EP, BLK], BF16) for u in range(2)]
    mask_tok = [sb(f"mask_tok{u}", [E, BLK]) for u in range(2)]
    x_in = [sb(f"xe_in{u}", [P, TPB, D]) for u in range(2)]
    z = [sb(f"z{u}", [P, TPB, D]) for u in range(2)]
    G = 4
    g = [sb(f"g{r}", [P, BLK]) for r in range(G)]
    bn = sb("bn_z", [P, TPB, 6])
    mv = sb("mv_z", [P, TPB, 2])
    var = sb("var_z", [P, TPB])
    rstd = sb("rstd_z", [P, TPB])
    h_ps = [ps(f"h_ps{r}", [P, BLK]) for r in range(2)]
    o_ps = [ps(f"o_ps{k}", [P, BLK])[:, 0:D] for k in range(TPB)]
    tok_all, stats = t["tok_all"], t["stats_all"]

    loaded = [sem(f"e_loaded{u}") for u in range(2)]
    LOADS = 4
    hidden = sem("e_hidden")
    gelu = sem("e_gelu")
    gated = sem("e_gated")
    used = sem("e_used")
    summed = sem("e_summed")
    z_done = sem("e_z")
    bn_done, mv_done, rstd_done, pool_chain = sem("e_bn"), sem("e_mv"), sem("e_rstd"), sem("e_pool")
    dve_chain = sem("e_dve")
    renormed = sem("e_renormed")
    scaled = sem("e_scaled")
    based = sem("e_based")

    with nc.Block() as block:
        @block.sync
        def _(sp):
            sp.dma_start(w2_sb[:, :, :], t["w2"].rearrange("(c p) n -> p c n", p=P)).then_inc(w2_loaded, 16)
            with sp.Fori(0, NBLK // 2) as i:
                for u in range(2):
                    blk = i * 2 + u
                    sp.wait_ge(based, blk + 2)
                    row, col = (blk // BPS) * E, (blk % BPS) * BLK
                    for k in range(2):
                        src = t["mask_b"].rearrange("(b e k) s -> b k e s", b=B, k=2)[ds(blk // BPS, 1), k, :, ds(col, BLK)]
                        sp.dma_start(mask_bc[u][k * F:(k + 1) * F, :, :],
                                     src.broadcast_to([F, EP, BLK])).then_inc(loaded[u], 16)
                    sp.dma_start(mask_tok[u][:, :], t["mask_f"][ds(row, E), ds(col, BLK)]).then_inc(loaded[u], 16)
                    sp.dma_start(x_in[u][:, :, :], t["x_blocks"][ds(blk, 1)].rearrange("n p t d -> (n p) t d")).then_inc(loaded[u], 16)

        @block.tensor
        def _(pe):
            pe.sem_inc(used, G)
            pe.wait_ge(w2_loaded, 16)

            def hide(blk, e):
                n = blk * EP + e
                pe.wait_ge(gelu, n + 1)
                for c in range(KC):
                    ins = pe.matmul(h_ps[e % 2][:, :], t["w1_sb"][:, c, e * P:(e + 1) * P],
                                    tok_all[:, ds(blk, 1), c * BLK:(c + 1) * BLK].rearrange("p n s -> p (n s)"),
                                    start=(c == 0), stop=(c == KC - 1))
                ins.then_inc(hidden, 1)

            def unhide(blk, e):
                pe.wait_ge(gated, blk * EP + e + 1)
                for k in range(TPB):
                    if e == 0:
                        pe.wait_ge(z_done, blk * TPB + k + 1)
                    ins = pe.matmul(o_ps[k], g[e % G][:, k * P:(k + 1) * P], w2_sb[:, e, :],
                                    start=(e == 0), stop=False)
                ins.then_inc(used, 1)

            with pe.Fori(0, NBLK // 2) as i:
                for u in range(2):
                    blk = i * 2 + u
                    hide(blk, 0)
                    for e in range(EP):
                        if e + 1 < EP:
                            hide(blk, e + 1)
                        unhide(blk, e)
                    pe.wait_ge(loaded[u], (i + 1) * 16 * LOADS)
                    for k in range(TPB):
                        pe.matmul(o_ps[k], mask_tok[u][:, k * P:(k + 1) * P], t["b2_sb"][:, :],
                                  start=False, stop=True).then_inc(summed, 1)

        @block.scalar
        def _(act):
            act.sem_inc(gelu, 2)
            with act.Fori(0, NBLK) as blk:
                for e in range(EP):
                    n = blk * EP + e
                    act.wait_ge(hidden, n + 1)
                    act.wait_ge(used, n + 1)
                    act.activation(g[e % G][:, :], h_ps[e % 2][:, :], ACT.Gelu, bias=t["b1_col"][:, e:e + 1]).then_inc(gelu, 1)

        @block.vector
        def _(dve):
            dve.sem_inc(z_done, TPB)

            def start_block(i, u, blk):
                dve.wait_ge(loaded[u], (i + 1) * 16 * LOADS)

            def gate(blk, u, e):
                n = blk * EP + e
                dve.wait_ge(gelu, n + 3)
                dve.tensor_tensor(g[e % G][:, :], g[e % G][:, :], mask_bc[u][:, e, :], ALU.mult).then_inc(gated, 1)

            def renormalise(blk, u):
                for k in range(TPB):
                    st = stats[:, ds(blk * TPB + k, 1), :].rearrange("p n s -> p (n s)")
                    ins = dve.tensor_scalar(z[u][:, k, :], x_in[u][:, k, :], st[:, 0:1], st[:, 1:2], ALU.subtract, ALU.mult)
                return ins

            def add_sum(blk, u):
                for k in range(TPB):
                    dve.wait_ge(summed, blk * TPB + k + 1)
                    dve.tensor_tensor(z[u][:, k, :], z[u][:, k, :], o_ps[k], ALU.add).then_inc(z_done, 1)

            def statistics(blk, u):
                dve.wait_ge(z_done, blk * TPB + 2 * TPB)
                for k in range(TPB):
                    ins = dve.bn_stats(bn[:, k, :], z[u][:, k, :])
                ins.then_inc(bn_done, 1)
                wait_apart(dve, bn_done, blk + 1, t["passed"][0])
                for k in range(TPB):
                    ins = dve.bn_aggr(mv[:, k, :], bn[:, k, :])
                ins.then_inc(mv_done, 1)

            def scale(blk, u):
                chain = Chain(dve, dve_chain, blk)
                dve.wait_ge(rstd_done, blk + 1)
                for k in range(TPB):
                    ins = dve.tensor_scalar(z[u][:, k, :], z[u][:, k, :], mv[:, k, 0:1], rstd[:, k:k + 1], ALU.subtract, ALU.mult)
                chain(ins)
                dve.tensor_tensor(z[u][:, :, :], z[u][:, :, :], t["gamma_bc"][:, :].unsqueeze(1).broadcast_to([P, TPB, D]),
                                  ALU.mult).then_inc(scaled, 1)

            def gates(blk, i, u, last):
                start_block(i, u, blk)
                for e in range(EP):
                    gate(blk, u, e)
                    if last and e == 0:
                        statistics(blk - 1, 1 - u)
                    if last and e == 3:
                        scale(blk - 1, 1 - u)
                if last:
                    dve.wait_ge(based, blk + 2)
                renormalise(blk, u).then_inc(renormed, 1)
                dve.wait_ge(renormed, blk + 1)
                add_sum(blk, u)

            gates(0, 0, 0, False)
            with dve.Fori(0, NBLK // 2 - 1) as i:
                gates(i * 2 + 1, i, 1, True)
                gates(i * 2 + 2, i + 1, 0, True)
            gates(NBLK - 1, NBLK // 2 - 1, 1, True)
            statistics(NBLK - 1, 1)
            scale(NBLK - 1, 1)

        @block.gpsimd
        def _(pool):
            pool.sem_inc(based, 3)
            with pool.Fori(0, NBLK // 2) as i:
                for u in range(2):
                    blk = i * 2 + u
                    chain = Chain(pool, pool_chain, blk * 2)
                    wait_apart(pool, mv_done, blk + 1, t["passed"][2])
                    chain(pool.tensor_scalar(var[:, :], mv[:, :, 1], EPS_LN, None, ALU.add))
                    pool.tensor_tensor(rstd[:, :], var[:, :], t["minus_half"][:, :], ALU.pow).then_inc(rstd_done, 1)
                    chain(pool.tensor_tensor(x_in[u][:, :, :], x_in[u][:, :, :],
                                             t["shift_bc"][:, :].unsqueeze(1).broadcast_to([P, TPB, D]), ALU.add))
                    pool.wait_ge(scaled, blk + 1)
                    pool.tensor_tensor(tok_all[:, ds(blk, 1), :].rearrange("p n (k d) -> p (n k) d", k=TPB),
                                       z[u][:, :, :], x_in[u][:, :, :], ALU.add).then_inc(based, 1)


def attend(nc, sem, sb, ps, t):
    R = 3
    q_feat = [sb(f"q_feat{r}", [FEAT + SHIFT, S], BF16) for r in range(R)]
    k_feat = [sb(f"k_feat{r}", [FEAT + SHIFT, S], BF16) for r in range(R)]
    prob = [sb(f"prob{r}", [P, S]) for r in range(R)]
    v_head = [sb(f"v_head{r}", [P, ST, VW]) for r in range(R)]
    att = [sb(f"att{r}", [P, BLK]) for r in range(R)]
    half_max = sb("half_max", [P, ST, 2])
    row_max = sb("row_max", [P, ST])
    left = sb("left", [P, ST])
    shift = sb("shift", [P, SHIFT, ST], BF16)
    shift_t = sb("shift_t", [SHIFT * ST, P], BF16)
    ident16 = sb("ident16", [P, P], BF16)
    s_ps = [ps(f"s_ps{r}", [P, BLK]) for r in range(R)]
    m_ps = [ps(f"m_ps{r}", [P, 2 * BLK]) for r in range(2)]
    a_ps = ps("a_ps", [P, BLK])
    QB = S // BLK
    PAIRS = ST * 2
    shift_ps = m_ps[0][:, :].bitcast(BF16)[0:SHIFT * ST, 0:P]

    fed = [sem(f"a_fed{r}") for r in range(R)]
    LOADS = len(Q_ORDER) + len(K_ORDER)
    piece = sem("a_piece")
    maxed = sem("a_maxed")
    shift_done = sem("a_shift")
    shift_turned = sem("a_turned")
    shift_read = sem("a_shift_read")
    shift_in = sem("a_shift_in")
    scored = sem("a_scored")
    exped = sem("a_exped")
    weighed = sem("a_weighed")
    v_ready = sem("a_v_ready")
    att_read = sem("a_att_read")
    att_out = [sem(f"a_att_out{r}") for r in range(R)]
    chain_sem = sem("a_chain")
    consts, consts16 = sem("a_consts"), sem("a_consts16")

    PLAN = [0] + [3, 2, 3] * 4 + [0] * 3
    assert sum(PLAN) == PAIRS and len(PLAN) == ST
    TURN_AT = 14

    with nc.Block() as block:
        @block.gpsimd
        def _(pool):
            for r in range(R):
                ins = pool.memset(v_head[r][:, :, :], 1.0)
            ins.then_inc(consts, 1)
            pool.wait_ge(consts, 1)

            def copy_v(n, r):
                pool.tensor_copy(v_head[r][:, :, 0:HD],
                                 t["v_all"][:, :, :, :, :].rearrange("p b h s d -> p (b h) s d")[:, ds(n, 1)].rearrange("p n s d -> p (n s) d")
                                 ).then_inc(v_ready, 1)

            for n in range(R):
                copy_v(n, n)
            with pool.Fori(0, (HEADS - R - 1) // R) as i:
                for r in range(R):
                    n = i * R + R + r
                    pool.wait_ge(weighed, (n - R + 1) * ST + 3)
                    copy_v(n, r)
            pool.wait_ge(weighed, (HEADS - R) * ST + 3)
            copy_v(HEADS - 1, (HEADS - 1) % R)

        @block.sync
        def _(sp):
            def feed(n, r):
                for parts, feat, order in ((t["q_parts"], q_feat[r], Q_ORDER), (t["k_parts"], k_feat[r], K_ORDER)):
                    at = 0
                    for first, count in order:
                        rows = parts[:, ds(n * HD, HD), :]
                        if parts is t["q_parts"]:
                            src = rows[first:first + 1].broadcast_to([count, HD, S])
                        else:
                            src = rows[first:first + count]
                        sp.dma_start(feat[at:at + count * HD, :], src).then_inc(fed[r], 16)
                        at += count * HD

            def put_shift(n, r):
                sp.wait_ge(shift_read, n + 1)
                sp.dma_start(q_feat[r][FEAT:FEAT + SHIFT, :].rearrange("k (q p) -> k q p", p=P),
                             shift_t[:, :]).then_inc(shift_in, 16)

            def put_att(g, r):
                sp.wait_ge(att_read, g + 2)
                sp.dma_start(t["att_dram"][ds(g, 1)].rearrange("n p s -> (n p) s"), att[r][:, :]).then_inc(att_out[r], 16)

            for r in range(R):
                sp.sem_inc(att_out[r], 16)
            for n in range(R):
                feed(n, n)
            put_shift(0, 0)
            def step(g, r, more=True):
                put_shift(g + 1, (r + 1) % R)
                if more:
                    sp.wait_ge(scored, (g + 1) * ST * QB)
                    feed(g + R, r)
                put_att(g, r)

            with sp.Fori(0, (HEADS - R - 1) // R) as i:
                for r in range(R):
                    step(i * R + r, r)
            for g in range(HEADS - R - 1, HEADS - 1):
                step(g, g % R, g + R < HEADS)
            put_att(HEADS - 1, (HEADS - 1) % R)
            for r in range(R):
                sp.wait_ge(att_out[r], 16 * (len(range(r, HEADS, R)) + 1))

        @block.scalar
        def _(act):
            act.sem_inc(exped, R)
            act.sem_inc(att_read, 1)

            def exps(g, it, r, kt):
                for qb in range(QB):
                    n = (g * ST + kt) * QB + qb
                    c = (r * ST + kt) * QB + qb
                    if qb == 0:
                        act.wait_ge(weighed, g * ST + kt + 1)
                    act.wait_ge(scored, n + 1)
                    act.activation(prob[(c // QB) % R][:, qb * BLK:(qb + 1) * BLK], s_ps[c % R][:, :], ACT.Exp).then_inc(exped, 1)

            def collect(g, it, r):
                act.wait_ge(weighed, (g + 1) * ST + 3)
                act.wait_ge(att_out[r], it * 16 + 16)
                act.activation(att[r][:, :], a_ps[:, :], ACT.Copy).then_inc(att_read, 1)

            exps(0, 0, 0, 0)
            with act.Fori(0, HEADS // R) as i:
                for r in range(R):
                    g = i * R + r
                    for kt in range(1, ST):
                        exps(g, i, r, kt)
                    exps(g + 1, i + (r + 1) // R, (r + 1) % R, 0)
                    collect(g, i, r)
            g = HEADS - 1
            for kt in range(1, ST):
                exps(g, g // R, g % R, kt)
            collect(g, g // R, g % R)

        @block.tensor
        def _(pe):
            pe.sem_inc(weighed, R)

            def pass1(n, r, p):
                pe.wait_ge(maxed, n * PAIRS + p + 1)
                qt, half = divmod(p, 2)
                for k in range(2):
                    key = half * 2 * BLK + k * BLK
                    ins = pe.matmul(m_ps[p % 2][:, k * BLK:(k + 1) * BLK], q_feat[r][0:FEAT, qt * P:(qt + 1) * P],
                                    k_feat[r][0:FEAT, key:key + BLK], start=True, stop=True)
                ins.then_inc(piece, 1)

            def turn(n):
                wait_apart(pe, shift_done, n + 1, t["passed"][1])
                pe.transpose(shift_ps, shift[:, :, :].rearrange("p k q -> p (k q)"), ident16[:, :]).then_inc(shift_turned, 1)

            def score(g, r, kt, qb):
                n = (g * ST + kt) * QB + qb
                c = (r * ST + kt) * QB + qb
                pe.wait_ge(exped, n + 1)
                pe.matmul(s_ps[c % R][:, :], k_feat[r][:, kt * P:(kt + 1) * P], q_feat[r][:, qb * BLK:(qb + 1) * BLK],
                          start=True, stop=True).then_inc(scored, 1)

            def weigh(g, r, kt):
                if kt == 0:
                    pe.wait_ge(v_ready, g + 1)
                    pe.wait_ge(att_read, g + 1)
                pe.wait_ge(exped, (g * ST + kt) * QB + QB + R)
                for qb in range(QB):
                    ins = pe.matmul(a_ps[qb * VW:(qb + 1) * VW, :], v_head[r][:, kt, :],
                                    prob[(r * ST + kt) % R][:, qb * BLK:(qb + 1) * BLK],
                                    start=(kt == 0), stop=(kt == ST - 1))
                ins.then_inc(weighed, 1)

            def fed_by(n, it):
                return (it + 1) * 16 * LOADS

            def key_tile(g, r, kt, last, pieces, nxt):
                todo = [lambda p=p: pass1(nxt[0], nxt[1], p) for p in pieces]
                score(g, r, kt, 0)
                for f in todo[:1]:
                    f()
                score(g, r, kt, 1)
                if last is not None:
                    weigh(*last)
                score(g, r, kt, 2)
                for f in todo[1:2]:
                    f()
                score(g, r, kt, 3)
                for f in todo[2:]:
                    f()

            def step(g, r, it, more=True):
                done, nr = 0, (r + 1) % R
                if more:
                    pe.wait_ge(fed[nr], fed_by(g + 1, it + (r + 1) // R))
                for kt in range(1, ST):
                    pieces = range(done, done + PLAN[kt]) if more else ()
                    done += PLAN[kt]
                    if more and kt == TURN_AT:
                        turn(g + 1)
                    key_tile(g, r, kt, (g, r, kt - 1), pieces, (g + 1, nr))
                if more:
                    pe.wait_ge(shift_in, (g + 2) * 16)
                    key_tile(g + 1, nr, 0, (g, r, ST - 1), (), None)
                else:
                    weigh(g, r, ST - 1)

            pe.wait_ge(consts16, 1)
            pe.wait_ge(fed[0], fed_by(0, 0))
            for p in range(PAIRS):
                pass1(0, 0, p)
            turn(0)
            pe.wait_ge(shift_in, 16)
            key_tile(0, 0, 0, None, (), None)
            with pe.Fori(0, HEADS // R) as i:
                for r in range(R):
                    step(i * R + r, r, i)
            step(HEADS - 1, (HEADS - 1) % R, (HEADS - 1) // R, False)

        @block.vector
        def _(dve):
            for r in range(R):
                dve.memset(k_feat[r][FEAT:FEAT + SHIFT, :], 1.0)
            dve.tensor_copy(ident16[:, :], t["ident"][:, :]).then_inc(consts16, 1)
            dve.sem_inc(maxed, 2)

            LINKS = 5

            def maxima(n):
                for p in range(PAIRS):
                    dve.wait_ge(piece, n * PAIRS + p + 1)
                    dve.tensor_reduce(half_max[:, p // 2, p % 2:p % 2 + 1], m_ps[p % 2][:, :], AX.X, ALU.max).then_inc(maxed, 1)
                dve.wait_ge(maxed, n * PAIRS + PAIRS + 2)
                do = Chain(dve, chain_sem, n * LINKS)
                do(dve.tensor_reduce(row_max[:, :], half_max[:, :, :], AX.X, ALU.max))
                do(dve.tensor_scalar(shift[:, 0, :], row_max[:, :], -1.0, None, ALU.mult))
                do(dve.scalar_tensor_tensor(left[:, :], row_max[:, :], -1.0, shift[:, 0, :], ALU.mult, ALU.subtract))
                do(dve.tensor_copy(shift[:, 1, :], left[:, :]))
                do(dve.tensor_tensor(left[:, :], left[:, :], shift[:, 1, :], ALU.subtract))
                dve.tensor_copy(shift[:, 2, :], left[:, :]).then_inc(shift_done, 1)
                dve.wait_ge(shift_turned, n + 1)
                dve.tensor_copy(shift_t[:, :], shift_ps).then_inc(shift_read, 1)

            maxima(0)
            with dve.Fori(1, HEADS) as n:
                maxima(n)


def output(nc, sem, sb, ps, t):
    num = [sb(f"num{u}", [P, KC, BLK]) for u in range(2)]
    den = [sb(f"den{u}", [P, KC, BLK]) for u in range(2)]
    res = [sb(f"res{u}", [P, TPB, D]) for u in range(2)]
    y_ps = [ps(f"y_ps{j}", [P, 2, D]) for j in range(4)]
    loaded = [sem(f"o_loaded{u}") for u in range(2)]
    stored = [sem(f"o_stored{u}") for u in range(2)]
    inverted, divided = sem("o_inverted"), sem("o_divided")
    projected = sem("o_projected")
    added = sem("o_added")

    with nc.Block() as block:
        @block.sync
        def _(sp):
            with sp.Fori(0, NBLK // 2) as i:
                for u in range(2):
                    blk = i * 2 + u
                    sp.wait_ge(projected, blk * 2 + 2)
                    for c in range(KC):
                        heads = t["att_dram"].rearrange("n (j r) s -> n j r s", j=BPS)
                        part = heads[ds((blk // BPS) * H + c * (H // KC), H // KC), ds(blk % BPS, 1)]
                        sp.dma_start(num[u][:, c, :], part[:, :, 0:HD, :].rearrange("n j r s -> (n j) r s")).then_inc(loaded[u], 16)
                        sp.dma_start(den[u][:, c, :], part[:, :, HD:2 * HD, :].rearrange("n j r s -> (n j) r s")).then_inc(loaded[u], 16)

        @block.vector
        def _(dve):
            dve.sem_inc(added, 4)

            def divide(blk, i, u):
                dve.wait_ge(loaded[u], (i + 1) * 64)
                dve.reciprocal(den[u][:, :, :], den[u][:, :, :]).then_inc(inverted, 1)
                dve.wait_ge(inverted, blk + 1)
                dve.tensor_tensor(num[u][:, :, :], num[u][:, :, :], den[u][:, :, :], ALU.mult).then_inc(divided, 1)

            def add(blk, i, u):
                dve.wait_ge(stored[u], i * 16 + 16)
                for j in range(2):
                    dve.wait_ge(projected, blk * 2 + j + 5)
                    dve.tensor_tensor(res[u][:, 2 * j:2 * j + 2, :], y_ps[2 * u + j][:, :, :],
                                      t["tok_all"][:, ds(blk, 1), 2 * j * D:(2 * j + 2) * D].rearrange("p n (k d) -> p (n k) d", k=2),
                                      ALU.add).then_inc(added, 1)

            divide(0, 0, 0)
            with dve.Fori(0, NBLK // 2 - 1) as i:
                divide(i * 2 + 1, i, 1)
                add(i * 2, i, 0)
                divide(i * 2 + 2, i + 1, 0)
                add(i * 2 + 1, i, 1)
            divide(NBLK - 1, NBLK // 2 - 1, 1)
            add(NBLK - 2, NBLK // 2 - 1, 0)
            add(NBLK - 1, NBLK // 2 - 1, 1)

        @block.tensor
        def _(pe):
            pe.sem_inc(projected, 4)
            with pe.Fori(0, NBLK // 2) as i:
                for u in range(2):
                    blk = i * 2 + u
                    pe.wait_ge(divided, blk + 1)
                    for j in range(2):
                        pe.wait_ge(added, blk * 2 + j + 1)
                        for k in range(2):
                            tok = (2 * j + k) * P
                            for c in range(KC):
                                ins = pe.matmul(y_ps[2 * u + j][:, k, :], num[u][:, c, tok:tok + P], t["woT_sb"][:, c, :],
                                                start=(c == 0), stop=(c == KC - 1))
                        ins.then_inc(projected, 1)

        @block.scalar
        def _(act):
            for u in range(2):
                act.sem_inc(stored[u], 16)
            with act.Fori(0, NBLK // 2) as i:
                for u in range(2):
                    blk = i * 2 + u
                    act.wait_ge(added, blk * 2 + 6)
                    act.dma_start(t["out_blocks"][ds(blk, 1)].rearrange("n p t d -> (n p) t d"), res[u][:, :, :]).then_inc(stored[u], 16)
            for u in range(2):
                act.wait_ge(stored[u], 16 * (NBLK // 2 + 1))


def kernel(**inputs):
    import numpy as np
    import concourse.bacc as bacc
    from concourse.bass_utils import run_bass_kernel_spmd

    get = {k: np.asarray(v) for k, v in inputs.items()}
    a = {
        "x": get["L0_attn_hidden_states"].reshape(TOKENS, D),
        **{w + "T": get[f"L0_attn_{n}"].T for w, n in (("wq", "Wq"), ("wk", "Wk"), ("wv", "Wv"), ("wo", "Wo"))},
        "bq": get["L0_attn_bq"].reshape(KC, P).T,
        "bk": get["L0_attn_bk"].reshape(KC, P).T,
        "bv": get["L0_attn_bv"], "bo": get["L0_attn_bo"],
        "wg": get["L0_ffn_wg"], "bg": get["L0_ffn_bg"],
        "w1": get["L0_ffn_w1"].transpose(1, 0, 2).reshape(D, E * F),
        "b1": get["L0_ffn_b1"].reshape(EP, P).T,
        "w2": get["L0_ffn_w2"].reshape(E * F, D), "b2": get["L0_ffn_b2"],
        "gamma": get["L0_ffn_gamma"], "beta": get["L0_ffn_beta"],
    }
    a = {k: np.ascontiguousarray(v) for k, v in a.items()}
    nc = bacc.Bacc("TRN2", target_bir_lowering=False, num_devices=1)
    args = {k: nc.dram_tensor(f"in_{k}", v.shape, F32, kind="ExternalInput").ap() for k, v in a.items()}
    args["out"] = nc.dram_tensor("out", (TOKENS, D), F32, kind="ExternalOutput").ap()
    build(nc, **args)
    r = run_bass_kernel_spmd(nc, [{f"in_{k}": v for k, v in a.items()}], core_ids=[0])
    return r.results[0]["out"].reshape(B, S, D)
```

```python
from contextlib import ExitStack

import concourse.bass as bass
from concourse import mybir
from concourse.alu_op_type import AluOpType as ALU

F32 = mybir.dt.float32
BF16 = mybir.dt.bfloat16
I32 = mybir.dt.int32
ACT = mybir.ActivationFunctionType
AX = mybir.AxisListType
ds = bass.ds

P = 128
B, S, D = 4, 2048, 256
H = 16
HD = D // H
E, F = 16, 64
TOPK_TOKENS = S // 2
TOKENS = B * S
TILES = TOKENS // P
BLK = 512
TPB = BLK // P
NBLK = TOKENS // BLK
BPS = S // BLK
ST = S // P
KC = D // P
EP = E // 2
HEADS = B * H
EPS_LN, EPS_GATE = 1e-5, 1e-6
SCALE = float(HD) ** -0.5
PARTS = 3
Q_ORDER = [(0, 3), (1, 2), (2, 1)]
K_ORDER = [(0, 3), (0, 2), (0, 1)]
FEAT = 6 * HD
SHIFT = PARTS
VW = 32


class Chain:

    def __init__(self, eng, sem, base=0):
        self.eng, self.sem, self.base, self.n = eng, sem, base, 0

    def __call__(self, ins):
        self.n += 1
        ins.then_inc(self.sem, 1)
        self.eng.wait_ge(self.sem, self.base + self.n)


def wait_apart(eng, sem, value, passed):
    eng.wait_ge(sem, value)
    eng.sem_inc(passed, 1)


def build(nc, x, wqT, wkT, wvT, woT, bq, bk, bv, bo, wg, bg, w1, b1, w2, b2, gamma, beta, out):
    top = ExitStack()
    with top:
        def sb(name, shape, dt=F32, ctx=top):
            return ctx.enter_context(nc.sbuf_tensor(name, shape, dt))

        def ps(name, shape, ctx):
            return ctx.enter_context(nc.psum_tensor(name, shape, F32))

        def sem(name):
            return top.enter_context(nc.semaphore(name))

        q_parts = nc.dram_tensor("q_parts", [PARTS, B * D, S], BF16).ap()
        k_parts = nc.dram_tensor("k_parts", [PARTS, B * D, S], BF16).ap()
        att_dram = nc.dram_tensor("att_dram", [HEADS, P, BLK], F32).ap()
        mask_f = nc.dram_tensor("mask_f", [B * E, S], F32).ap()
        mask_b = nc.dram_tensor("mask_b", [B * E, S], BF16).ap()
        inverse_dram = nc.dram_tensor("inverse_dram", [HEADS * BPS, BLK], F32).ap()

        passed = [sem(f"passed_{e}") for e in ("dve", "pe", "pool")]
        x_blocks = x.rearrange("(n t p) d -> n p t d", p=P, t=TPB)
        out_blocks = out.rearrange("(n t p) d -> n p t d", p=P, t=TPB)

        tok_all = sb("tok_all", [P, NBLK, KC * BLK])
        v_all = sb("v_all", [P, B, H, ST, HD])
        woT_sb = sb("woT_sb", [P, KC, D])
        ident = sb("ident", [P, P])
        warm = sb("warm", [P, 1])

        setup_stage = ExitStack()
        early = setup_stage
        with early:
            w1_sb = sb("w1_sb", [P, KC, E * F], ctx=early)
            b2_sb = sb("b2_sb", [E, D], ctx=early)
            b1_col = sb("b1_col", [P, EP], ctx=early)
            gamma_bc = sb("gamma_bc", [P, D], ctx=early)
            shift_bc = sb("shift_bc", [P, D], ctx=early)
            stats_all = sb("stats_all", [P, TILES, 2], ctx=early)
            minus_half = sb("minus_half", [P, TPB], ctx=early)

            mid = ExitStack()
            with mid:
                wqT_sb = sb("wqT_sb", [P, KC, D], ctx=mid)
                wkT_sb = sb("wkT_sb", [P, KC, D], ctx=mid)
                wvg_sb = sb("wvg_sb", [P, KC, D + E], ctx=mid)
                bg_bc = sb("bg_bc", [P, E], ctx=mid)
                bv_bc = sb("bv_bc", [P, D], ctx=mid)
                bq_col = sb("bq_col", [P, KC], ctx=mid)
                bqs_col = sb("bqs_col", [P, KC], ctx=mid)
                bk_col = sb("bk_col", [P, KC], ctx=mid)
                logits = sb("logits", [P, TILES, E], ctx=mid)
                with ExitStack() as st:
                    bo_bc = sb("bo_bc", [P, D], ctx=st)
                    setup(nc, sem, locals())
                with ExitStack() as st:
                    norm(nc, sem, lambda *a: sb(*a, ctx=st), lambda *a: ps(*a, ctx=st), locals())
                with ExitStack() as st:
                    project(nc, sem, lambda *a: sb(*a, ctx=st), lambda *a: ps(*a, ctx=st), locals())
            with ExitStack() as st:
                experts(nc, sem, lambda *a: sb(*a, ctx=st), lambda *a: ps(*a, ctx=st), locals())
        with ExitStack() as st:
            attend(nc, sem, lambda *a: sb(*a, ctx=st), lambda *a: ps(*a, ctx=st), locals())
        with ExitStack() as st:
            output(nc, sem, lambda *a: sb(*a, ctx=st), lambda *a: ps(*a, ctx=st), locals())


def setup(nc, sem, t):
    loaded, made, base = sem("setup_loaded"), sem("setup_made"), sem("setup_sum")
    with nc.Block() as block:
        @block.sync
        def _(sp):
            loads = [(dst, t[w].rearrange("(c p) n -> p c n", p=P)) for w, dst in
                     (("wvT", t["wvg_sb"][:, :, 0:D]), ("wg", t["wvg_sb"][:, :, D:D + E]),
                      ("wqT", t["wqT_sb"][:, :, :]), ("wkT", t["wkT_sb"][:, :, :]),
                      ("woT", t["woT_sb"][:, :, :]), ("w1", t["w1_sb"][:, :, :]))]
            loads.append((t["b2_sb"][:, :], t["b2"]))
            loads += [(t[c][:, :], t[a]) for c, a in (("b1_col", "b1"), ("bq_col", "bq"), ("bk_col", "bk"))]
            loads += [(t[c][:, :], t[a].partition_broadcast(P)) for c, a in
                      (("gamma_bc", "gamma"), ("shift_bc", "beta"), ("bo_bc", "bo"),
                       ("bg_bc", "bg"), ("bv_bc", "bv"))]
            for dst, src in loads:
                sp.dma_start(dst, src).then_inc(loaded, 16)
            sp.wait_ge(loaded, 16 * len(loads))
            sp.sem_inc(base, 1)

        @block.gpsimd
        def _(pool):
            pool.memset(t["ident"][:, :], 0.0).then_inc(made, 1)
            pool.memset(t["minus_half"][:, :], -0.5)
            pool.wait_ge(made, 1)
            pool.affine_select(out=t["ident"][:, :], in_=t["ident"][:, :], compare_op=ALU.not_equal,
                               fill=1.0, base=0, pattern=[[-1, P]], channel_multiplier=1)

        @block.vector
        def _(dve):
            dve.wait_ge(base, 1)
            dve.tensor_tensor(t["shift_bc"][:, :], t["shift_bc"][:, :], t["bo_bc"][:, :], ALU.add)
            dve.tensor_scalar(t["bqs_col"][:, :], t["bq_col"][:, :], SCALE, None, ALU.mult)


def norm(nc, sem, sb, ps, t):
    x_in = [sb(f"x_in{u}", [P, TPB, D]) for u in range(2)]
    xn = [sb(f"xn{u}", [P, TPB, D]) for u in range(2)]
    xT = [sb(f"xT{u}", [P, KC, BLK]) for u in range(2)]
    bn = [sb(f"bn{u}", [P, TPB, 6]) for u in range(2)]
    mv = [sb(f"mv{u}", [P, TPB, 2]) for u in range(2)]
    var = [sb(f"var{u}", [P, TPB]) for u in range(2)]
    rstd = [sb(f"rstd{u}", [P, TPB]) for u in range(2)]
    xT_ps = [ps(f"xT_ps{c}", [P, BLK]) for c in range(KC)]
    vg_ps = ps("vg_ps", [P, TPB, BLK])
    logits, v_all, tok_all, stats = t["logits"], t["v_all"], t["tok_all"], t["stats_all"]
    v_view = v_all[:, :, :, :, :].rearrange("p b h s d -> p b s h d")

    x_loaded = [sem(f"n_x_loaded{u}") for u in range(2)]
    bn_done, mv_done, rstd_done = sem("n_bn"), sem("n_mv"), sem("n_rstd")
    pool_chain = sem("n_pool")
    xn_done = sem("n_xn")
    transposed = sem("n_transposed")
    xT_copied = sem("n_xT")
    ps_freed = sem("n_ps_freed")
    projected = sem("n_projected")
    taken = sem("n_taken")
    logits_taken = sem("n_logits_taken")

    with nc.Block() as block:
        @block.sync
        def _(sp):
            with sp.Fori(0, NBLK // 2) as i:
                for u in range(2):
                    blk = i * 2 + u
                    sp.wait_ge(xn_done, blk + 1)
                    sp.dma_start(x_in[u][:, :, :], t["x_blocks"][ds(blk, 1)].rearrange("n p t d -> (n p) t d")).then_inc(x_loaded[u], 16)

        @block.vector
        def _(dve):
            dve.sem_inc(xn_done, 2)
            dve.sem_inc(taken, TPB)
            dve.sem_inc(logits_taken, 1)

            def statistics(blk, i, u):
                dve.wait_ge(x_loaded[u], i * 16 + 16)
                dve.wait_ge(rstd_done, blk + 1)
                for k in range(TPB):
                    ins = dve.bn_stats(bn[u][:, k, :], x_in[u][:, k, :])
                ins.then_inc(bn_done, 1)
                wait_apart(dve, bn_done, blk + 1, t["passed"][0])
                for k in range(TPB):
                    ins = dve.bn_aggr(mv[u][:, k, :], bn[u][:, k, :])
                ins.then_inc(mv_done, 1)

            def scale(blk, u):
                dve.wait_ge(rstd_done, blk + 3)
                dve.wait_ge(transposed, blk * 2 + 1)
                for k in range(TPB):
                    ins = dve.tensor_scalar(xn[u][:, k, :], x_in[u][:, k, :], mv[u][:, k, 0:1],
                                            rstd[u][:, k:k + 1], ALU.subtract, ALU.mult)
                ins.then_inc(xn_done, 1)

            def take(blk):
                for k in range(TPB):
                    dve.wait_ge(projected, blk * TPB + k + 1 + 2 * TPB)
                    dve.tensor_tensor(
                        v_view[:, ds(blk // BPS, 1), ds((blk % BPS) * TPB + k, 1), :, :].rearrange("p b s h d -> p (b s h) d"),
                        vg_ps[:, k, 0:D].rearrange("p (h d) -> p h d", h=H),
                        t["bv_bc"][:, :].rearrange("p (h d) -> p h d", h=H), ALU.add).then_inc(taken, 1)
                dve.tensor_tensor(logits[:, ds(blk * TPB, TPB), :], vg_ps[:, :, D:D + E],
                                  t["bg_bc"][:, :].unsqueeze(1).broadcast_to([P, TPB, E]),
                                  ALU.add).then_inc(logits_taken, 1)

            statistics(0, 0, 0)
            scale(0, 0)
            statistics(1, 0, 1)
            scale(1, 1)
            statistics(2, 1, 0)
            scale(2, 0)
            statistics(3, 1, 1)
            with dve.Fori(0, (NBLK - 4) // 2) as i:
                for k in range(2):
                    turn = i * 2 + 1 + k
                    take(turn - 1)
                    scale(turn + 2, 1 - k)
                    statistics(turn + 3, i + 2, k)
            take(NBLK - 4)
            scale(NBLK - 1, 1)
            for blk in range(NBLK - 3, NBLK):
                take(blk)

        @block.gpsimd
        def _(pool):
            pool.sem_inc(rstd_done, 2)
            with pool.Fori(0, NBLK // 2) as i:
                for u in range(2):
                    blk = i * 2 + u
                    wait_apart(pool, mv_done, blk + 1, t["passed"][2])
                    pool.tensor_scalar(var[u][:, :], mv[u][:, :, 1], EPS_LN, None, ALU.add).then_inc(pool_chain, 1)
                    pool.tensor_copy(stats[:, ds(blk * TPB, TPB), 0], mv[u][:, :, 0])
                    pool.wait_ge(pool_chain, blk + 1)
                    pool.tensor_tensor(rstd[u][:, :], var[u][:, :], t["minus_half"][:, :], ALU.pow).then_inc(rstd_done, 1)
                    pool.wait_ge(rstd_done, blk + 3)
                    pool.tensor_copy(stats[:, ds(blk * TPB, TPB), 1], rstd[u][:, :])

        @block.scalar
        def _(act):
            act.activation(t["warm"][:, :], t["ident"][:, 0:1], ACT.Copy)
            act.sem_inc(ps_freed, 2)
            with act.Fori(0, NBLK // 2) as i:
                for u in range(2):
                    blk = i * 2 + u
                    for c in range(KC):
                        act.wait_ge(transposed, blk * 2 + c + 3)
                        if c == 0:
                            act.wait_ge(projected, blk * TPB + 1)
                        act.activation(xT[u][:, c, :], xT_ps[c][:, :], ACT.Copy).then_inc(xT_copied, 1)
                        act.activation(tok_all[:, ds(blk, 1), c * BLK:(c + 1) * BLK].rearrange("p n s -> p (n s)"),
                                       xT_ps[c][:, :], ACT.Copy).then_inc(ps_freed, 1)

        @block.tensor
        def _(pe):
            pe.sem_inc(transposed, 2)
            pe.sem_inc(projected, 2 * TPB)

            def transpose(blk, u):
                pe.wait_ge(xn_done, blk + 3)
                for c in range(KC):
                    pe.wait_ge(ps_freed, blk * 2 + c + 1)
                    for k in range(TPB):
                        ins = pe.transpose(xT_ps[c][:, k * P:(k + 1) * P], xn[u][:, k, c * P:(c + 1) * P], t["ident"][:, :])
                    ins.then_inc(transposed, 1)

            def project_tokens(blk, u):
                pe.wait_ge(xT_copied, blk * 2 + 2)
                for k in range(TPB):
                    pe.wait_ge(taken, blk * TPB + k + 1)
                    if k == 0:
                        pe.wait_ge(logits_taken, blk + 1)
                    for c in range(KC):
                        ins = pe.matmul(vg_ps[:, k, 0:D + E], xT[u][:, c, k * P:(k + 1) * P], t["wvg_sb"][:, c, :],
                                        start=(c == 0), stop=(c == KC - 1))
                    ins.then_inc(projected, 1)

            transpose(0, 0)
            with pe.Fori(0, NBLK // 2 - 1) as i:
                for k in range(2):
                    transpose(i * 2 + k + 1, 1 - k)
                    project_tokens(i * 2 + k, k)
            transpose(NBLK - 1, 1)
            project_tokens(NBLK - 2, 0)
            project_tokens(NBLK - 1, 1)


def project(nc, sem, sb, ps, t):
    M = 2 * KC
    f32s = [sb(f"f32s{m}", [P, BLK]) for m in range(M)]
    rest = [sb(f"rest{m}", [P, BLK]) for m in range(M)]
    parts = [sb(f"parts{m}", [P, PARTS, BLK], BF16) for m in range(M)]
    qk_ps = [ps(f"qk_ps{m}", [P, BLK]) for m in range(M)]
    route_ps = ps("route_ps", [B * E, S])
    weights = [t["wqT_sb"], t["wqT_sb"], t["wkT_sb"], t["wkT_sb"]]
    biases = [t["bqs_col"], t["bqs_col"], t["bk_col"], t["bk_col"]]
    scales = [SCALE, SCALE, 1.0, 1.0]
    targets = [t["q_parts"], t["q_parts"], t["k_parts"], t["k_parts"]]

    scored = sem("p_scored")
    first = sem("p_first")
    rest_done = sem("p_rest")
    second = sem("p_second")
    third = sem("p_third")
    stored = [sem(f"p_stored{m}") for m in range(M)]
    shifted, exped = sem("p_shifted"), sem("p_exped")
    routed, route_t = sem("p_routed"), sem("p_route_t")
    masked, mask_stored = sem("p_masked"), sem("p_mask_stored")
    chain = sem("p_chain")
    loop_chain = sem("p_loop_chain")

    lg = t["logits"]
    work = sb("work", [P, 4, TILES, E])
    ex, tmp, hot, hot2 = (work[:, k] for k in range(4))
    red = sb("red", [P, TILES])
    order_i = sb("order_i", [P, E], I32)
    order = sb("order", [P, E])
    denom = sb("denom", [P, ST, E])
    gt = sb("gt", [B * E, S])
    junk = gt[:, 0:S // 2].bitcast(BF16)
    eq, cum = (work[0:B * E, 2 * k:2 * k + 2].rearrange("p k n e -> p (k n e)") for k in range(2))
    mask16 = cum[:, 0:S // 2].bitcast(BF16)
    bit = sb("bit", [B * E, 1], I32)
    cand = sb("cand", [B * E, 1], I32)
    drop = sb("drop", [B * E, 1], I32)
    count = sb("count", [B * E, 1])
    need = sb("need", [B * E, 1])
    ordered = sem("p_ordered")

    with nc.Block() as block:
        @block.tensor
        def _(pe):
            def chunks(lo, hi):
                with pe.Fori(lo, hi) as blk:
                    for m in range(M):
                        pe.wait_ge(first, blk * M + m + 1)
                        for c in range(KC):
                            half = m % KC
                            ins = pe.matmul(qk_ps[m][:, :], weights[m][:, c, half * P:(half + 1) * P],
                                            t["tok_all"][:, ds(blk, 1), c * BLK:(c + 1) * BLK].rearrange("p n s -> p (n s)"),
                                            start=(c == 0), stop=(c == KC - 1))
                        ins.then_inc(scored, 1)

            chunks(0, NBLK // 4)
            pe.wait_ge(routed, 1)
            for s in range(ST):
                ins = pe.transpose(route_ps[:, s * P:(s + 1) * P], tmp[:, s * B:(s + 1) * B, :].rearrange("p b e -> p (b e)"),
                                   t["ident"][:, :])
            ins.then_inc(route_t, 1)
            chunks(NBLK // 4, NBLK)

        @block.scalar
        def _(act):
            act.sem_inc(first, M)
            act.wait_ge(shifted, 1)
            act.activation(ex[:, :, :], lg[:, :, :], ACT.Exp).then_inc(exped, 1)

            def take_first(n, m, blk):
                act.wait_ge(scored, n + 1)
                act.wait_ge(rest_done, n + 1)
                act.activation(f32s[m][:, :], qk_ps[m][:, :], ACT.Identity, bias=biases[m][:, m % KC:m % KC + 1], scale=scales[m])
                act.wait_ge(stored[m], blk * 16 + 16)
                act.activation(parts[m][:, 0, :], qk_ps[m][:, :], ACT.Identity, bias=biases[m][:, m % KC:m % KC + 1],
                               scale=scales[m]).then_inc(first, 1)

            def take_second(n, m):
                act.wait_ge(rest_done, n + 1 + M)
                act.activation(parts[m][:, 1, :], rest[m][:, :], ACT.Copy).then_inc(second, 1)

            take_first(0, 0, 0)
            with act.Fori(0, NBLK - 1) as blk:
                for m in range(M):
                    take_first(blk * M + m + 1, (m + 1) % M, blk + (m + 1) // M)
                    take_second(blk * M + m, m)
            last = (NBLK - 1) * M
            for m in range(M):
                if m + 1 < M:
                    take_first(last + m + 1, m + 1, NBLK - 1)
                take_second(last + m, m)
            act.wait_ge(masked, 1)
            act.dma_start(t["mask_f"], gt[:, :]).then_inc(mask_stored, 16)
            act.dma_start(t["mask_b"], mask16).then_inc(mask_stored, 16)
            act.wait_ge(mask_stored, 32)

        @block.gpsimd
        def _(pool):
            pool.sem_inc(rest_done, M)
            pool.sem_inc(third, M)
            pool.iota(order_i[:, :], pattern=[[-1, E]], base=E, channel_multiplier=0).then_inc(ordered, 1)

            def take_rest(n, m):
                pool.wait_ge(first, n + 1 + M)
                pool.wait_ge(third, n + 1)
                pool.tensor_tensor(rest[m][:, :], f32s[m][:, :], parts[m][:, 0, :], ALU.subtract).then_inc(rest_done, 1)

            def take_third(n, m):
                pool.wait_ge(second, n + 1)
                pool.tensor_tensor(parts[m][:, 2, :], rest[m][:, :], parts[m][:, 1, :], ALU.subtract).then_inc(third, 1)

            take_rest(0, 0)
            with pool.Fori(0, NBLK - 1) as blk:
                for m in range(M):
                    take_rest(blk * M + m + 1, (m + 1) % M)
                    take_third(blk * M + m, m)
            last = (NBLK - 1) * M
            for m in range(M):
                if m + 1 < M:
                    take_rest(last + m + 1, m + 1)
                take_third(last + m, m)

        @block.sync
        def _(sp):
            for m in range(M):
                sp.sem_inc(stored[m], 16)
            with sp.Fori(0, NBLK) as blk:
                for m in range(M):
                    sp.wait_ge(third, blk * M + m + 1 + M)
                    row = (blk // BPS) * D + (m % KC) * P
                    sp.dma_start(targets[m][:, ds(row, P), ds((blk % BPS) * BLK, BLK)].rearrange("r p s -> p r s"),
                                 parts[m][:, :, :]).then_inc(stored[m], 16)
            for m in range(M):
                sp.wait_ge(stored[m], 16 * NBLK + 16)

        @block.vector
        def _(dve):
            do = Chain(dve, chain)
            wide = lambda a: a[:, :].unsqueeze(2).broadcast_to([P, TILES, E])
            do(dve.tensor_reduce(red[:, :], lg[:, :, :], AX.X, ALU.max))
            dve.tensor_tensor(lg[:, :, :], lg[:, :, :], wide(red), ALU.subtract).then_inc(shifted, 1)
            dve.wait_ge(exped, 1)
            do(dve.tensor_reduce(red[:, :], ex[:, :, :], AX.X, ALU.add))
            do(dve.reciprocal(red[:, :], red[:, :]))
            do(dve.tensor_tensor(ex[:, :, :], ex[:, :, :], wide(red), ALU.mult))
            dve.wait_ge(ordered, 1)
            do(dve.tensor_copy(order[:, :], order_i[:, :]))
            order_bc = order[:, :].unsqueeze(1).broadcast_to([P, TILES, E])
            scores = ex
            for k, h in enumerate((hot, hot2)):
                do(dve.tensor_reduce(red[:, :], scores[:, :, :], AX.X, ALU.max))
                do(dve.tensor_tensor(h[:, :, :], scores[:, :, :], wide(red), ALU.is_equal))
                do(dve.tensor_tensor(h[:, :, :], h[:, :, :], order_bc, ALU.mult))
                do(dve.tensor_reduce(red[:, :], h[:, :, :], AX.X, ALU.max))
                do(dve.tensor_tensor(h[:, :, :], h[:, :, :], wide(red), ALU.is_equal))
                if k == 0:
                    do(dve.scalar_tensor_tensor(tmp[:, :, :], hot[:, :, :], -4.0, ex[:, :, :], ALU.mult, ALU.add))
                    scores = tmp
            do(dve.tensor_tensor(hot[:, :, :], hot[:, :, :], hot2[:, :, :], ALU.add))
            do(dve.tensor_tensor(ex[:, :, :], ex[:, :, :], hot[:, :, :], ALU.mult))
            by_batch = ex[:, :, :].rearrange("p (b s) e -> p b s e", b=B)
            do(dve.tensor_tensor(denom[:, :, :], by_batch[:, 0], by_batch[:, 1], ALU.add))
            for b in range(2, B):
                do(dve.tensor_tensor(denom[:, :, :], denom[:, :, :], by_batch[:, b], ALU.add))
            do(dve.tensor_scalar(denom[:, :, :], denom[:, :, :], EPS_GATE, None, ALU.add))
            do(dve.reciprocal(denom[:, :, :], denom[:, :, :]))
            routes = tmp[:, :, :].rearrange("p (s b) e -> p b s e", b=B)
            for b in range(B):
                do(dve.scalar_tensor_tensor(routes[:, b], by_batch[:, b], float(B), denom[:, :, :], ALU.mult, ALU.mult))
            do(dve.memset(cand[:, :], 1 << 30))
            dve.memset(bit[:, :], 1 << 30).then_inc(routed, 1)
            dve.wait_ge(route_t, 1)

            STEP = 5
            with dve.Fori(0, 31) as i:
                step = Chain(dve, loop_chain, i * STEP)
                step(dve.tensor_scalar(junk, route_ps[:, :], cand[:, :].bitcast(F32), None, ALU.is_ge, ALU.add,
                                       accum_out=count[:, :]))
                step(dve.tensor_scalar(drop[:, :], count[:, :], TOPK_TOKENS - 0.5, -1.0, ALU.is_lt, ALU.mult))
                step(dve.tensor_tensor(drop[:, :], drop[:, :], bit[:, :], ALU.bitwise_and))
                step(dve.tensor_scalar(bit[:, :], bit[:, :], 1, None, ALU.logical_shift_right))
                step(dve.scalar_tensor_tensor(cand[:, :], cand[:, :], drop[:, :], bit[:, :], ALU.bitwise_xor, ALU.bitwise_or))
            bound = cand[:, :].bitcast(F32)
            do(dve.tensor_scalar(gt[:, :], route_ps[:, :], bound, None, ALU.is_gt, ALU.add, accum_out=count[:, :]))
            do(dve.tensor_scalar(need[:, :], count[:, :], -1.0, float(TOPK_TOKENS), ALU.mult, ALU.add))
            do(dve.tensor_scalar(eq[:, :], route_ps[:, :], bound, None, ALU.is_equal))
            do(dve.tensor_tensor_scan(cum[:, :], eq[:, :], eq[:, :], 0.0, ALU.add, ALU.max))
            do(dve.scalar_tensor_tensor(eq[:, :], cum[:, :], need[:, :], eq[:, :], ALU.is_le, ALU.mult))
            do(dve.tensor_tensor(gt[:, :], gt[:, :], eq[:, :], ALU.add))
            dve.tensor_copy(mask16, gt[:, :]).then_inc(masked, 1)


def experts(nc, sem, sb, ps, t):
    w2_sb = sb("w2_sb", [P, EP, D])
    w2_loaded = sem("e_w2_loaded")
    mask_bc = [sb(f"mask_bc{u}", [P, EP, BLK], BF16) for u in range(2)]
    mask_tok = [sb(f"mask_tok{u}", [E, BLK]) for u in range(2)]
    x_in = [sb(f"xe_in{u}", [P, TPB, D]) for u in range(2)]
    z = [sb(f"z{u}", [P, TPB, D]) for u in range(2)]
    G = 4
    g = [sb(f"g{r}", [P, BLK]) for r in range(G)]
    bn = sb("bn_z", [P, TPB, 6])
    mv = sb("mv_z", [P, TPB, 2])
    var = sb("var_z", [P, TPB])
    rstd = sb("rstd_z", [P, TPB])
    h_ps = [ps(f"h_ps{r}", [P, BLK]) for r in range(2)]
    o_ps = [ps(f"o_ps{k}", [P, BLK])[:, 0:D] for k in range(TPB)]
    tok_all, stats = t["tok_all"], t["stats_all"]

    loaded = [sem(f"e_loaded{u}") for u in range(2)]
    LOADS = 4
    hidden = sem("e_hidden")
    gelu = sem("e_gelu")
    gated = sem("e_gated")
    used = sem("e_used")
    summed = sem("e_summed")
    z_done = sem("e_z")
    bn_done, mv_done, rstd_done, pool_chain = sem("e_bn"), sem("e_mv"), sem("e_rstd"), sem("e_pool")
    dve_chain = sem("e_dve")
    renormed = sem("e_renormed")
    scaled = sem("e_scaled")
    based = sem("e_based")

    with nc.Block() as block:
        @block.sync
        def _(sp):
            sp.dma_start(w2_sb[:, :, :], t["w2"].rearrange("(c p) n -> p c n", p=P)).then_inc(w2_loaded, 16)
            with sp.Fori(0, NBLK // 2) as i:
                for u in range(2):
                    blk = i * 2 + u
                    sp.wait_ge(based, blk + 2)
                    row, col = (blk // BPS) * E, (blk % BPS) * BLK
                    for k in range(2):
                        src = t["mask_b"].rearrange("(b e k) s -> b k e s", b=B, k=2)[ds(blk // BPS, 1), k, :, ds(col, BLK)]
                        sp.dma_start(mask_bc[u][k * F:(k + 1) * F, :, :],
                                     src.broadcast_to([F, EP, BLK])).then_inc(loaded[u], 16)
                    sp.dma_start(mask_tok[u][:, :], t["mask_f"][ds(row, E), ds(col, BLK)]).then_inc(loaded[u], 16)
                    sp.dma_start(x_in[u][:, :, :], t["x_blocks"][ds(blk, 1)].rearrange("n p t d -> (n p) t d")).then_inc(loaded[u], 16)

        @block.tensor
        def _(pe):
            pe.sem_inc(used, G)
            pe.wait_ge(w2_loaded, 16)

            def hide(blk, e):
                n = blk * EP + e
                pe.wait_ge(gelu, n + 1)
                for c in range(KC):
                    ins = pe.matmul(h_ps[e % 2][:, :], t["w1_sb"][:, c, e * P:(e + 1) * P],
                                    tok_all[:, ds(blk, 1), c * BLK:(c + 1) * BLK].rearrange("p n s -> p (n s)"),
                                    start=(c == 0), stop=(c == KC - 1))
                ins.then_inc(hidden, 1)

            def unhide(blk, e):
                pe.wait_ge(gated, blk * EP + e + 1)
                for k in range(TPB):
                    if e == 0:
                        pe.wait_ge(z_done, blk * TPB + k + 1)
                    ins = pe.matmul(o_ps[k], g[e % G][:, k * P:(k + 1) * P], w2_sb[:, e, :],
                                    start=(e == 0), stop=False)
                ins.then_inc(used, 1)

            with pe.Fori(0, NBLK // 2) as i:
                for u in range(2):
                    blk = i * 2 + u
                    hide(blk, 0)
                    for e in range(EP):
                        if e + 1 < EP:
                            hide(blk, e + 1)
                        unhide(blk, e)
                    pe.wait_ge(loaded[u], (i + 1) * 16 * LOADS)
                    for k in range(TPB):
                        pe.matmul(o_ps[k], mask_tok[u][:, k * P:(k + 1) * P], t["b2_sb"][:, :],
                                  start=False, stop=True).then_inc(summed, 1)

        @block.scalar
        def _(act):
            act.activation(t["warm"][:, :], t["ident"][:, 0:1], ACT.Gelu)
            act.sem_inc(gelu, 2)
            with act.Fori(0, NBLK) as blk:
                for e in range(EP):
                    n = blk * EP + e
                    act.wait_ge(hidden, n + 1)
                    act.wait_ge(used, n + 1)
                    act.activation(g[e % G][:, :], h_ps[e % 2][:, :], ACT.Gelu, bias=t["b1_col"][:, e:e + 1]).then_inc(gelu, 1)

        @block.vector
        def _(dve):
            dve.sem_inc(z_done, TPB)

            def start_block(i, u, blk):
                dve.wait_ge(loaded[u], (i + 1) * 16 * LOADS)

            def gate(blk, u, e):
                n = blk * EP + e
                dve.wait_ge(gelu, n + 3)
                dve.tensor_tensor(g[e % G][:, :], g[e % G][:, :], mask_bc[u][:, e, :], ALU.mult).then_inc(gated, 1)

            def renormalise(blk, u):
                for k in range(TPB):
                    st = stats[:, ds(blk * TPB + k, 1), :].rearrange("p n s -> p (n s)")
                    ins = dve.tensor_scalar(z[u][:, k, :], x_in[u][:, k, :], st[:, 0:1], st[:, 1:2], ALU.subtract, ALU.mult)
                return ins

            def add_sum(blk, u):
                for k in range(TPB):
                    dve.wait_ge(summed, blk * TPB + k + 1)
                    dve.tensor_tensor(z[u][:, k, :], z[u][:, k, :], o_ps[k], ALU.add).then_inc(z_done, 1)

            def statistics(blk, u):
                dve.wait_ge(z_done, blk * TPB + 2 * TPB)
                for k in range(TPB):
                    ins = dve.bn_stats(bn[:, k, :], z[u][:, k, :])
                ins.then_inc(bn_done, 1)
                wait_apart(dve, bn_done, blk + 1, t["passed"][0])
                for k in range(TPB):
                    ins = dve.bn_aggr(mv[:, k, :], bn[:, k, :])
                ins.then_inc(mv_done, 1)

            def scale(blk, u):
                chain = Chain(dve, dve_chain, blk)
                dve.wait_ge(rstd_done, blk + 1)
                for k in range(TPB):
                    ins = dve.tensor_scalar(z[u][:, k, :], z[u][:, k, :], mv[:, k, 0:1], rstd[:, k:k + 1], ALU.subtract, ALU.mult)
                chain(ins)
                dve.tensor_tensor(z[u][:, :, :], z[u][:, :, :], t["gamma_bc"][:, :].unsqueeze(1).broadcast_to([P, TPB, D]),
                                  ALU.mult).then_inc(scaled, 1)

            def gates(blk, i, u, last):
                start_block(i, u, blk)
                for e in range(EP):
                    gate(blk, u, e)
                    if last and e == 0:
                        statistics(blk - 1, 1 - u)
                    if last and e == 3:
                        scale(blk - 1, 1 - u)
                if last:
                    dve.wait_ge(based, blk + 2)
                renormalise(blk, u).then_inc(renormed, 1)
                dve.wait_ge(renormed, blk + 1)
                add_sum(blk, u)

            gates(0, 0, 0, False)
            with dve.Fori(0, NBLK // 2 - 1) as i:
                gates(i * 2 + 1, i, 1, True)
                gates(i * 2 + 2, i + 1, 0, True)
            gates(NBLK - 1, NBLK // 2 - 1, 1, True)
            statistics(NBLK - 1, 1)
            scale(NBLK - 1, 1)

        @block.gpsimd
        def _(pool):
            pool.sem_inc(based, 3)
            with pool.Fori(0, NBLK // 2) as i:
                for u in range(2):
                    blk = i * 2 + u
                    chain = Chain(pool, pool_chain, blk * 2)
                    wait_apart(pool, mv_done, blk + 1, t["passed"][2])
                    chain(pool.tensor_scalar(var[:, :], mv[:, :, 1], EPS_LN, None, ALU.add))
                    pool.tensor_tensor(rstd[:, :], var[:, :], t["minus_half"][:, :], ALU.pow).then_inc(rstd_done, 1)
                    chain(pool.tensor_tensor(x_in[u][:, :, :], x_in[u][:, :, :],
                                             t["shift_bc"][:, :].unsqueeze(1).broadcast_to([P, TPB, D]), ALU.add))
                    pool.wait_ge(scaled, blk + 1)
                    pool.tensor_tensor(tok_all[:, ds(blk, 1), :].rearrange("p n (k d) -> p (n k) d", k=TPB),
                                       z[u][:, :, :], x_in[u][:, :, :], ALU.add).then_inc(based, 1)


def attend(nc, sem, sb, ps, t):
    R = 3
    q_feat = [sb(f"q_feat{r}", [FEAT + SHIFT, S], BF16) for r in range(R)]
    k_feat = [sb(f"k_feat{r}", [FEAT + SHIFT, S], BF16) for r in range(R)]
    prob = [sb(f"prob{r}", [P, S]) for r in range(R)]
    v_head = [sb(f"v_head{r}", [P, ST, VW]) for r in range(R)]
    att = [sb(f"att{r}", [P, BLK]) for r in range(R)]
    half_max = [sb(f"half_max{r}", [P, ST, 2]) for r in range(R)]
    row_max = [sb(f"row_max{r}", [P, ST]) for r in range(R)]
    left = sb("left", [P, ST])
    minus_one = sb("minus_one", [P, ST])
    shift = sb("shift", [P, SHIFT, ST], BF16)
    shift_t = sb("shift_t", [SHIFT * ST, P], BF16)
    ident16 = sb("ident16", [P, P], BF16)
    s_ps = [ps(f"s_ps{r}", [P, BLK]) for r in range(R)]
    m_ps = [ps(f"m_ps{r}", [P, 2 * BLK]) for r in range(2)]
    a_ps = ps("a_ps", [P, BLK])
    QB = S // BLK
    PAIRS = ST * 2
    shift_ps = m_ps[0][:, :].bitcast(BF16)[0:SHIFT * ST, 0:P]

    fed = [sem(f"a_fed{r}") for r in range(R)]
    LOADS = len(Q_ORDER) + len(K_ORDER)
    piece = sem("a_piece")
    maxed = sem("a_maxed")
    row_maxed = sem("a_row_maxed")
    shift_done = sem("a_shift")
    shift_turned = sem("a_turned")
    shift_read = sem("a_shift_read")
    shift_in = sem("a_shift_in")
    scored = sem("a_scored")
    exped = sem("a_exped")
    weighed = sem("a_weighed")
    v_ready = sem("a_v_ready")
    att_read = sem("a_att_read")
    att_out = [sem(f"a_att_out{r}") for r in range(R)]
    chain_sem = sem("a_chain")
    sums_in, sums_inverted = sem("a_sums_in"), sem("a_sums_inverted")
    sums = sb("sums", [P, BLK])
    consts, consts16 = sem("a_consts"), sem("a_consts16")

    PER = 2
    EARLY = 5 * PER
    AFTER = ST - 4
    assert EARLY + (AFTER - 1) * PER == PAIRS
    TURN_AT = AFTER + 2
    TURN_PIECE = (TURN_AT - AFTER) * PER
    LINKS = 4

    with nc.Block() as block:
        @block.gpsimd
        def _(pool):
            for r in range(R):
                pool.memset(v_head[r][:, :, :], 1.0)
            pool.memset(minus_one[:, :], -1.0).then_inc(consts, 1)
            pool.wait_ge(consts, 1)

            def copy_v(n, r):
                pool.tensor_copy(v_head[r][:, :, 0:HD],
                                 t["v_all"][:, :, :, :, :].rearrange("p b h s d -> p (b h) s d")[:, ds(n, 1)].rearrange("p n s d -> p (n s) d")
                                 ).then_inc(v_ready, 1)

            def split_shift(n, r):
                pool.wait_ge(row_maxed, n + 1)
                if not (isinstance(n, int) and n == 0):
                    pool.wait_ge(shift_turned, n)
                do = Chain(pool, chain_sem, n * LINKS)
                do(pool.tensor_tensor(shift[:, 0, :], row_max[r][:, :], minus_one[:, :], ALU.mult))
                do(pool.tensor_tensor(left[:, :], row_max[r][:, :], shift[:, 0, :], ALU.add))
                do(pool.tensor_tensor(shift[:, 1, :], left[:, :], minus_one[:, :], ALU.mult))
                do(pool.tensor_tensor(left[:, :], left[:, :], shift[:, 1, :], ALU.add))
                pool.tensor_tensor(shift[:, 2, :], left[:, :], minus_one[:, :], ALU.mult).then_inc(shift_done, 1)

            for n in range(R):
                copy_v(n, n)
            split_shift(0, 0)
            with pool.Fori(0, (HEADS - R - 1) // R) as i:
                for r in range(R):
                    n = i * R + R + r
                    split_shift(n - R + 1, (r + 1) % R)
                    pool.wait_ge(weighed, (n - R + 1) * ST + 3)
                    copy_v(n, r)
            for n in range(HEADS - 1, HEADS + R - 1):
                split_shift(n - R + 1, (n + 1) % R)
                if n < HEADS:
                    pool.wait_ge(weighed, (n - R + 1) * ST + 3)
                    copy_v(n, n % R)

        @block.sync
        def _(sp):
            def feed(n, r):
                for parts, feat, order in ((t["q_parts"], q_feat[r], Q_ORDER), (t["k_parts"], k_feat[r], K_ORDER)):
                    at = 0
                    for first, count in order:
                        rows = parts[:, ds(n * HD, HD), :]
                        if parts is t["q_parts"]:
                            src = rows[first:first + 1].broadcast_to([count, HD, S])
                        else:
                            src = rows[first:first + count]
                        sp.dma_start(feat[at:at + count * HD, :], src).then_inc(fed[r], 16)
                        at += count * HD

            def put_shift(n, r):
                sp.wait_ge(shift_read, n + 1)
                sp.dma_start(q_feat[r][FEAT:FEAT + SHIFT, :].rearrange("k (q p) -> k q p", p=P),
                             shift_t[:, :]).then_inc(shift_in, 16)

            def put_att(g, r):
                sp.wait_ge(att_read, g + 2)
                sp.dma_start(t["att_dram"][ds(g, 1)].rearrange("n p s -> (n p) s"), att[r][:, :]).then_inc(att_out[r], 16)

            for r in range(R):
                sp.sem_inc(att_out[r], 16)
            for n in range(R):
                feed(n, n)
            put_shift(0, 0)
            def step(g, r, more=True):
                put_shift(g + 1, (r + 1) % R)
                if more:
                    sp.wait_ge(scored, (g + 1) * ST * QB)
                    feed(g + R, r)
                put_att(g, r)

            with sp.Fori(0, (HEADS - R - 1) // R) as i:
                for r in range(R):
                    step(i * R + r, r)
            for g in range(HEADS - R - 1, HEADS - 1):
                step(g, g % R, g + R < HEADS)
                if g == HEADS - R:
                    for r in range(R):
                        sp.wait_ge(att_out[r], 16 * (HEADS // 2 // R + 2))
                    sp.dma_start(sums[:, :], sum_rows(t, 0)).then_inc(sums_in, 16)
            put_att(HEADS - 1, (HEADS - 1) % R)
            sp.wait_ge(sums_inverted, 1)
            sp.dma_start(t["inverse_dram"][0:P, :], sums[:, :]).then_inc(sums_in, 16)
            sp.wait_ge(sums_in, 32)
            for r in range(R):
                sp.wait_ge(att_out[r], 16 * (len(range(r, HEADS, R)) + 1))

        @block.scalar
        def _(act):
            act.sem_inc(exped, R)
            act.sem_inc(att_read, 1)

            def exps(g, it, r, kt, shift_of=None):
                for qb in range(QB):
                    n = (g * ST + kt) * QB + qb
                    c = (r * ST + kt) * QB + qb
                    if kt == TURN_AT - 1 and qb == QB - 1 and shift_of is not None:
                        read_shift(shift_of)
                    if qb == 0:
                        act.wait_ge(weighed, g * ST + kt + 1)
                    act.wait_ge(scored, n + 1)
                    act.activation(prob[(c // QB) % R][:, qb * BLK:(qb + 1) * BLK], s_ps[c % R][:, :], ACT.Exp).then_inc(exped, 1)

            def read_shift(n):
                act.wait_ge(shift_turned, n + 1)
                act.activation(shift_t[:, :], shift_ps, ACT.Copy).then_inc(shift_read, 1)

            def collect(g, it, r):
                act.wait_ge(weighed, (g + 1) * ST + 3)
                act.wait_ge(att_out[r], it * 16 + 16)
                act.activation(att[r][:, :], a_ps[:, :], ACT.Copy).then_inc(att_read, 1)

            read_shift(0)
            exps(0, 0, 0, 0)
            with act.Fori(0, HEADS // R) as i:
                for r in range(R):
                    g = i * R + r
                    for kt in range(1, ST):
                        exps(g, i, r, kt, g + 1)
                    exps(g + 1, i + (r + 1) // R, (r + 1) % R, 0)
                    collect(g, i, r)
            g = HEADS - 1
            for kt in range(1, ST):
                exps(g, g // R, g % R, kt)
            collect(g, g // R, g % R)

        @block.tensor
        def _(pe):
            pe.sem_inc(weighed, R)

            def pass1(n, r, p, shift_before=True):
                pe.wait_ge(maxed, n * PAIRS + p + 1)
                if p == TURN_PIECE and shift_before:
                    pe.wait_ge(shift_read, n)
                qt, half = divmod(p, 2)
                for k in range(2):
                    key = half * 2 * BLK + k * BLK
                    ins = pe.matmul(m_ps[p % 2][:, k * BLK:(k + 1) * BLK], q_feat[r][0:FEAT, qt * P:(qt + 1) * P],
                                    k_feat[r][0:FEAT, key:key + BLK], start=True, stop=True)
                ins.then_inc(piece, 1)

            def turn(n, more=True):
                if more:
                    pe.wait_ge(maxed, (n + 1) * PAIRS + TURN_PIECE - 1 + 2)
                wait_apart(pe, shift_done, n + 1, t["passed"][1])
                pe.transpose(shift_ps, shift[:, :, :].rearrange("p k q -> p (k q)"), ident16[:, :]).then_inc(shift_turned, 1)

            def score(g, r, kt, qb):
                n = (g * ST + kt) * QB + qb
                c = (r * ST + kt) * QB + qb
                pe.wait_ge(exped, n + 1)
                pe.matmul(s_ps[c % R][:, :], k_feat[r][:, kt * P:(kt + 1) * P], q_feat[r][:, qb * BLK:(qb + 1) * BLK],
                          start=True, stop=True).then_inc(scored, 1)

            def weigh(g, r, kt):
                if kt == 0:
                    pe.wait_ge(v_ready, g + 1)
                    pe.wait_ge(att_read, g + 1)
                pe.wait_ge(exped, (g * ST + kt) * QB + QB + R)
                for qb in range(QB):
                    ins = pe.matmul(a_ps[qb * VW:(qb + 1) * VW, :], v_head[r][:, kt, :],
                                    prob[(r * ST + kt) % R][:, qb * BLK:(qb + 1) * BLK],
                                    start=(kt == 0), stop=(kt == ST - 1))
                ins.then_inc(weighed, 1)

            def wait_fed(r, it):
                pe.wait_ge(fed[r % R], (it + r // R + 1) * 16 * LOADS)

            def key_tile(g, r, kt, last, pieces, late=False, between=lambda: None):
                first, second = [lambda p=p: pass1(*p) for p in pieces] or [lambda: None] * 2
                score(g, r, kt, 0)
                if not late:
                    first()
                score(g, r, kt, 1)
                if late:
                    first()
                else:
                    second()
                score(g, r, kt, 2)
                if last is not None:
                    weigh(*last)
                if late:
                    second()
                between()
                score(g, r, kt, 3)

            def step(g, r, it, following=True, after=True):
                nr, ar = (r + 1) % R, (r + 2) % R
                for kt in range(1, AFTER):
                    p = EARLY + (kt - 1) * PER
                    pieces = [(g + 1, nr, p + k) for k in range(PER)] if following else []
                    key_tile(g, r, kt, (g, r, kt - 1), pieces)
                if after:
                    wait_fed(r + 2, it)
                early = [[(g + 2, ar, j * PER + k) for k in range(PER)] if after else [] for j in range(EARLY // PER)]
                for j, kt in enumerate(range(AFTER, ST)):
                    turns = following and kt == TURN_AT - 1
                    key_tile(g, r, kt, (g, r, kt - 1), early[j], late=(kt == TURN_AT),
                             **({"between": lambda: turn(g + 1, after)} if turns else {}))
                if following:
                    pe.wait_ge(shift_in, (g + 2) * 16)
                    key_tile(g + 1, nr, 0, (g, r, ST - 1), early[-1])
                else:
                    weigh(g, r, ST - 1)

            pe.wait_ge(consts16, 1)
            wait_fed(0, 0)
            for p in range(PAIRS):
                pass1(0, 0, p, shift_before=False)
            wait_fed(1, 0)
            for p in range(EARLY):
                if p == TURN_PIECE:
                    turn(0)
                pass1(1, 1, p)
            pe.wait_ge(shift_in, 16)
            key_tile(0, 0, 0, None, [])
            rounds = (HEADS - 2) // R
            with pe.Fori(0, rounds) as i:
                for r in range(R):
                    step(i * R + r, r, i)
            for g in range(rounds * R, HEADS):
                step(g, g % R, g // R, following=g + 1 < HEADS, after=g + 2 < HEADS)

        @block.vector
        def _(dve):
            for r in range(R):
                dve.memset(k_feat[r][FEAT:FEAT + SHIFT, :], 1.0)
            dve.tensor_copy(ident16[:, :], t["ident"][:, :]).then_inc(consts16, 1)
            dve.sem_inc(maxed, 2)

            def maxima(n, r):
                for p in range(PAIRS):
                    dve.wait_ge(piece, n * PAIRS + p + 1)
                    if p == 0 and not (isinstance(n, int) and n < R):
                        dve.wait_ge(shift_done, n - R + 1)
                    dve.tensor_reduce(half_max[r][:, p // 2, p % 2:p % 2 + 1], m_ps[p % 2][:, :], AX.X, ALU.max).then_inc(maxed, 1)
                dve.wait_ge(maxed, n * PAIRS + PAIRS + 2)
                dve.tensor_reduce(row_max[r][:, :], half_max[r][:, :, :], AX.X, ALU.max).then_inc(row_maxed, 1)

            for n in range(R):
                maxima(n, n)
            with dve.Fori(1, HEADS // R) as i:
                for r in range(R):
                    maxima(i * R + r, r)
            maxima(HEADS - 1, (HEADS - 1) % R)
            dve.wait_ge(sums_in, 16)
            dve.reciprocal(sums[:, :], sums[:, :]).then_inc(sums_inverted, 1)


def sum_rows(t, half):
    return t["att_dram"].rearrange("n (j r) s -> (n j) r s", r=VW)[half * P:(half + 1) * P, HD, :]


def output(nc, sem, sb, ps, t):
    num = [sb(f"num{u}", [P, KC, BLK]) for u in range(2)]
    inv = [sb(f"inv{u}", [P, KC, BLK]) for u in range(2)]
    sums = sb("sums2", [P, BLK])
    sums_in, sums_inverted = sem("o_sums_in"), sem("o_sums_inverted")
    res = [sb(f"res{u}", [P, TPB, D]) for u in range(2)]
    y_ps = [ps(f"y_ps{j}", [P, 2, D]) for j in range(4)]
    loaded = [sem(f"o_loaded{u}") for u in range(2)]
    stored = [sem(f"o_stored{u}") for u in range(2)]
    divided = sem("o_divided")
    projected = sem("o_projected")
    added = sem("o_added")

    with nc.Block() as block:
        @block.sync
        def _(sp):
            sp.dma_start(sums[:, :], sum_rows(t, 1)).then_inc(sums_in, 16)
            sums_at = t["att_dram"].rearrange("n (j r) s -> n j r s", j=BPS)
            inverses = t["inverse_dram"].rearrange("(n j) s -> n j s", j=BPS)

            def load(blk, u):
                sp.wait_ge(projected, blk * 2 + 2)
                for c in range(KC):
                    heads, j = ds((blk // BPS) * H + c * (H // KC), H // KC), ds(blk % BPS, 1)
                    sp.dma_start(num[u][:, c, :], sums_at[heads, j, 0:HD, :].rearrange("n j r s -> (n j) r s")).then_inc(loaded[u], 16)
                    sp.dma_start(inv[u][:, c, :], inverses[heads, j, :].broadcast_to([H // KC, HD, BLK])).then_inc(loaded[u], 16)

            load(0, 0)
            load(1, 1)
            sp.wait_ge(sums_inverted, 1)
            sp.dma_start(t["inverse_dram"][P:2 * P, :], sums[:, :]).then_inc(sums_in, 16)
            with sp.Fori(1, NBLK // 4) as i:
                for u in range(2):
                    load(i * 2 + u, u)
            sp.wait_ge(sums_in, 32)
            with sp.Fori(NBLK // 4, NBLK // 2) as i:
                for u in range(2):
                    load(i * 2 + u, u)

        @block.vector
        def _(dve):
            dve.sem_inc(added, 4)

            def divide(blk, i, u):
                dve.wait_ge(loaded[u], (i + 1) * 64)
                dve.tensor_tensor(num[u][:, :, :], num[u][:, :, :], inv[u][:, :, :], ALU.mult).then_inc(divided, 1)

            def add(blk, i, u):
                dve.wait_ge(stored[u], i * 16 + 16)
                for j in range(2):
                    dve.wait_ge(projected, blk * 2 + j + 5)
                    dve.tensor_tensor(res[u][:, 2 * j:2 * j + 2, :], y_ps[2 * u + j][:, :, :],
                                      t["tok_all"][:, ds(blk, 1), 2 * j * D:(2 * j + 2) * D].rearrange("p n (k d) -> p (n k) d", k=2),
                                      ALU.add).then_inc(added, 1)

            divide(0, 0, 0)
            dve.wait_ge(sums_in, 16)
            dve.reciprocal(sums[:, :], sums[:, :]).then_inc(sums_inverted, 1)
            with dve.Fori(0, NBLK // 2 - 1) as i:
                divide(i * 2 + 1, i, 1)
                add(i * 2, i, 0)
                divide(i * 2 + 2, i + 1, 0)
                add(i * 2 + 1, i, 1)
            divide(NBLK - 1, NBLK // 2 - 1, 1)
            add(NBLK - 2, NBLK // 2 - 1, 0)
            add(NBLK - 1, NBLK // 2 - 1, 1)

        @block.tensor
        def _(pe):
            pe.sem_inc(projected, 4)
            with pe.Fori(0, NBLK // 2) as i:
                for u in range(2):
                    blk = i * 2 + u
                    pe.wait_ge(divided, blk + 1)
                    for j in range(2):
                        pe.wait_ge(added, blk * 2 + j + 1)
                        for k in range(2):
                            tok = (2 * j + k) * P
                            for c in range(KC):
                                ins = pe.matmul(y_ps[2 * u + j][:, k, :], num[u][:, c, tok:tok + P], t["woT_sb"][:, c, :],
                                                start=(c == 0), stop=(c == KC - 1))
                        ins.then_inc(projected, 1)

        @block.scalar
        def _(act):
            for u in range(2):
                act.sem_inc(stored[u], 16)
            with act.Fori(0, NBLK // 2) as i:
                for u in range(2):
                    blk = i * 2 + u
                    act.wait_ge(added, blk * 2 + 6)
                    act.dma_start(t["out_blocks"][ds(blk, 1)].rearrange("n p t d -> (n p) t d"), res[u][:, :, :]).then_inc(stored[u], 16)
            for u in range(2):
                act.wait_ge(stored[u], 16 * (NBLK // 2 + 1))


def kernel(**inputs):
    import numpy as np
    import concourse.bacc as bacc
    from concourse.bass_utils import run_bass_kernel_spmd

    get = {k: np.asarray(v) for k, v in inputs.items()}
    a = {
        "x": get["L0_attn_hidden_states"].reshape(TOKENS, D),
        **{w + "T": get[f"L0_attn_{n}"].T for w, n in (("wq", "Wq"), ("wk", "Wk"), ("wv", "Wv"), ("wo", "Wo"))},
        "bq": get["L0_attn_bq"].reshape(KC, P).T,
        "bk": get["L0_attn_bk"].reshape(KC, P).T,
        "bv": get["L0_attn_bv"], "bo": get["L0_attn_bo"],
        "wg": get["L0_ffn_wg"], "bg": get["L0_ffn_bg"],
        "w1": get["L0_ffn_w1"].transpose(1, 0, 2).reshape(D, E * F),
        "b1": get["L0_ffn_b1"].reshape(EP, P).T,
        "w2": get["L0_ffn_w2"].reshape(E * F, D), "b2": get["L0_ffn_b2"],
        "gamma": get["L0_ffn_gamma"], "beta": get["L0_ffn_beta"],
    }
    a = {k: np.ascontiguousarray(v) for k, v in a.items()}
    nc = bacc.Bacc("TRN2", target_bir_lowering=False, num_devices=1)
    args = {k: nc.dram_tensor(f"in_{k}", v.shape, F32, kind="ExternalInput").ap() for k, v in a.items()}
    args["out"] = nc.dram_tensor("out", (TOKENS, D), F32, kind="ExternalOutput").ap()
    build(nc, **args)
    r = run_bass_kernel_spmd(nc, [{f"in_{k}": v for k, v in a.items()}], core_ids=[0])
    return r.results[0]["out"].reshape(B, S, D)
```

```python
from contextlib import ExitStack

import concourse.bass as bass
from concourse import mybir
from concourse.alu_op_type import AluOpType as ALU

F32 = mybir.dt.float32
BF16 = mybir.dt.bfloat16
I32 = mybir.dt.int32
F32R = mybir.dt.float32r
RING = 4
ACT = mybir.ActivationFunctionType
AX = mybir.AxisListType
ds = bass.ds

P = 128
B, S, D = 4, 2048, 256
H = 16
HD = D // H
E, F = 16, 64
TOPK_TOKENS = S // 2
TOKENS = B * S
TILES = TOKENS // P
BLK = 512
TPB = BLK // P
NBLK = TOKENS // BLK
BPS = S // BLK
ST = S // P
KC = D // P
EP = E // 2
HEADS = B * H
EPS_LN, EPS_GATE = 1e-5, 1e-6
SCALE = float(HD) ** -0.5
PARTS = 3
Q_ORDER = [(0, 3), (1, 2), (2, 1)]
K_ORDER = [(0, 3), (0, 2), (0, 1)]
FEAT = 6 * HD
SHIFT = PARTS
VW = 32


class Chain:

    def __init__(self, eng, sem, base=0):
        self.eng, self.sem, self.base, self.n = eng, sem, base, 0

    def __call__(self, ins):
        self.n += 1
        ins.then_inc(self.sem, 1)
        self.eng.wait_ge(self.sem, self.base + self.n)


def wait_apart(eng, sem, value, passed):
    eng.wait_ge(sem, value)
    eng.sem_inc(passed, 1)


def build(nc, x, wqT, wkT, wvT, woT, bq, bk, bv, bo, wg, bg, w1, b1, w2, b2, gamma, beta, out):
    top = ExitStack()
    with top:
        def sb(name, shape, dt=F32, ctx=top):
            return ctx.enter_context(nc.sbuf_tensor(name, shape, dt))

        def ps(name, shape, ctx):
            return ctx.enter_context(nc.psum_tensor(name, shape, F32))

        def sem(name):
            return top.enter_context(nc.semaphore(name))

        q_parts = nc.dram_tensor("q_parts", [PARTS, B * D, S], BF16).ap()
        k_parts = nc.dram_tensor("k_parts", [PARTS, B * D, S], BF16).ap()
        att_dram = nc.dram_tensor("att_dram", [HEADS, P, BLK], F32).ap()
        mask_b = nc.dram_tensor("mask_b", [B * E, S], BF16).ap()
        inverse_dram = nc.dram_tensor("inverse_dram", [HEADS * BPS, PARTS, BLK], BF16).ap()

        passed = [sem(f"passed_{e}") for e in ("dve", "pe", "pool")]
        x_blocks = x.rearrange("(n t p) d -> n p t d", p=P, t=TPB)
        out_blocks = out.rearrange("(n t p) d -> n p t d", p=P, t=TPB)

        tok_all = sb("tok_all", [P, NBLK, KC * BLK])
        v_all = sb("v_all", [P, B, H, ST, HD])
        ident = sb("ident", [P, P])
        warm = sb("warm", [P, 1])

        early = ExitStack()
        with early:
            b2_rows = sb("b2_rows", [PARTS * E, D], BF16, ctx=early)
            b1_col = sb("b1_col", [P, EP], ctx=early)
            gamma_bc = sb("gamma_bc", [P, D], ctx=early)
            shift_bc = sb("shift_bc", [P, D], ctx=early)
            stats_all = sb("stats_all", [P, TILES, 2], ctx=early)
            minus_half = sb("minus_half", [P, TPB], ctx=early)

            mid = ExitStack()
            with mid:
                wqT_sb = sb("wqT_sb", [P, KC, D], ctx=mid)
                wkT_sb = sb("wkT_sb", [P, KC, D], ctx=mid)
                wvg_sb = sb("wvg_sb", [P, KC, D + E], ctx=mid)
                bg_bc = sb("bg_bc", [P, E], ctx=mid)
                bv_bc = sb("bv_bc", [P, D], ctx=mid)
                bq_col = sb("bq_col", [P, KC], ctx=mid)
                bqs_col = sb("bqs_col", [P, KC], ctx=mid)
                bk_col = sb("bk_col", [P, KC], ctx=mid)
                logits = sb("logits", [P, TILES, E], ctx=mid)
                with ExitStack() as st:
                    norm(nc, sem, lambda *a: sb(*a, ctx=st), lambda *a: ps(*a, ctx=st), locals())
                with ExitStack() as st:
                    project(nc, sem, lambda *a: sb(*a, ctx=st), lambda *a: ps(*a, ctx=st), locals())
            with ExitStack() as st:
                experts(nc, sem, lambda *a: sb(*a, ctx=st), lambda *a: ps(*a, ctx=st), locals())
        num_ring = [sb("num0", [P, KC, BLK])]
        inv_ring = [sb("inv0", [H * PARTS, BLK], BF16)]
        inv_parts = sb("inv_parts", [P, PARTS, BLK], BF16)
        spread = sb("spread", [H * PARTS, D], BF16)
        woT_sb = sb("woT_sb", [P, KC, D])
        out_loaded = [sem(f"o_loaded{u}") for u in range(RING)]
        with ExitStack() as st:
            attend(nc, sem, lambda *a: sb(*a, ctx=st), lambda *a: ps(*a, ctx=st), locals())
        with ExitStack() as st:
            num_ring += [sb(f"num{u}", [P, KC, BLK], F32, st) for u in range(1, RING)]
            inv_ring += [sb(f"inv{u}", [H * PARTS, BLK], BF16, st) for u in range(1, RING)]
            output(nc, sem, lambda *a: sb(*a, ctx=st), lambda *a: ps(*a, ctx=st), locals())


def norm(nc, sem, sb, ps, t):
    x_in = [sb(f"x_in{u}", [P, TPB, D]) for u in range(2)]
    xn = [sb(f"xn{u}", [P, TPB, D]) for u in range(2)]
    xT = [sb(f"xT{u}", [P, KC, BLK]) for u in range(2)]
    bn = [sb(f"bn{u}", [P, TPB, 6]) for u in range(2)]
    mv = [sb(f"mv{u}", [P, TPB, 2]) for u in range(2)]
    var = [sb(f"var{u}", [P, TPB]) for u in range(2)]
    rstd = [sb(f"rstd{u}", [P, TPB]) for u in range(2)]
    xT_ps = [ps(f"xT_ps{c}", [P, BLK]) for c in range(KC)]
    vg_ps = ps("vg_ps", [P, TPB, BLK])
    logits, v_all, tok_all, stats = t["logits"], t["v_all"], t["tok_all"], t["stats_all"]
    v_view = v_all[:, :, :, :, :].rearrange("p b h s d -> p b s h d")

    x_loaded = [sem(f"n_x_loaded{u}") for u in range(2)]
    bn_done, mv_done, rstd_done = sem("n_bn"), sem("n_mv"), sem("n_rstd")
    pool_chain = sem("n_pool")
    xn_done = sem("n_xn")
    transposed = sem("n_transposed")
    xT_copied = sem("n_xT")
    ps_freed = sem("n_ps_freed")
    projected = sem("n_projected")
    taken = sem("n_taken")
    logits_taken = sem("n_logits_taken")

    bo_bc = sb("bo_bc", [P, D])
    b2_sb = sb("b2_sb", [E, D])
    b2_left = sb("b2_left", [E, D])
    b2_parts = sb("b2_parts", [E, PARTS, D], BF16)
    by_chunk = lambda w: t[w].rearrange("(c p) n -> p c n", p=P)
    now = [(t["wvg_sb"][:, :, 0:D], by_chunk("wvT")), (t["wvg_sb"][:, :, D:D + E], by_chunk("wg")),
           (t["bg_bc"][:, :], t["bg"].partition_broadcast(P)), (t["bv_bc"][:, :], t["bv"].partition_broadcast(P))]
    later = [(b2_sb[:, :], t["b2"]), (t["wqT_sb"][:, :, :], by_chunk("wqT")), (t["wkT_sb"][:, :, :], by_chunk("wkT"))]
    later += [(t[c][:, :], t[a]) for c, a in (("b1_col", "b1"), ("bq_col", "bq"), ("bk_col", "bk"))]
    later += [(t[c][:, :], t[a].partition_broadcast(P)) for c, a in (("gamma_bc", "gamma"), ("shift_bc", "beta"))]
    later.append((bo_bc[:, :], t["bo"].partition_broadcast(P)))
    now_in, later_in = sem("n_now_in"), sem("n_later_in")
    cleared, ident_made = sem("n_cleared"), sem("n_ident_made")
    b2_split, b2_chain, b2_placed = sem("n_b2_split"), sem("n_b2_chain"), sem("n_b2_placed")

    with nc.Block() as block:
        @block.sync
        def _(sp):
            with sp.Fori(0, NBLK // 2) as i:
                for u in range(2):
                    blk = i * 2 + u
                    sp.wait_ge(xn_done, blk + 1)
                    sp.dma_start(x_in[u][:, :, :], t["x_blocks"][ds(blk, 1)].rearrange("n p t d -> (n p) t d")).then_inc(x_loaded[u], 16)
            sp.wait_ge(b2_split, 1)
            for k in range(PARTS):
                sp.dma_start(t["b2_rows"][k * E:(k + 1) * E, :], b2_parts[:, k, :]).then_inc(b2_placed, 16)
            sp.wait_ge(b2_placed, 16 * PARTS)

        @block.vector
        def _(dve):
            dve.sem_inc(xn_done, 2)
            dve.sem_inc(taken, TPB)
            dve.sem_inc(logits_taken, 1)

            def statistics(blk, i, u):
                dve.wait_ge(x_loaded[u], i * 16 + 16)
                dve.wait_ge(rstd_done, blk + 1)
                for k in range(TPB):
                    ins = dve.bn_stats(bn[u][:, k, :], x_in[u][:, k, :])
                ins.then_inc(bn_done, 1)
                wait_apart(dve, bn_done, blk + 1, t["passed"][0])
                for k in range(TPB):
                    ins = dve.bn_aggr(mv[u][:, k, :], bn[u][:, k, :])
                ins.then_inc(mv_done, 1)

            def scale(blk, u):
                dve.wait_ge(rstd_done, blk + 3)
                dve.wait_ge(transposed, blk * 2 + 1)
                for k in range(TPB):
                    ins = dve.tensor_scalar(xn[u][:, k, :], x_in[u][:, k, :], mv[u][:, k, 0:1],
                                            rstd[u][:, k:k + 1], ALU.subtract, ALU.mult)
                ins.then_inc(xn_done, 1)

            def take(blk):
                for k in range(TPB):
                    dve.wait_ge(projected, blk * TPB + k + 1 + 2 * TPB)
                    dve.tensor_tensor(
                        v_view[:, ds(blk // BPS, 1), ds((blk % BPS) * TPB + k, 1), :, :].rearrange("p b s h d -> p (b s h) d"),
                        vg_ps[:, k, 0:D].rearrange("p (h d) -> p h d", h=H),
                        t["bv_bc"][:, :].rearrange("p (h d) -> p h d", h=H), ALU.add).then_inc(taken, 1)
                dve.tensor_tensor(logits[:, ds(blk * TPB, TPB), :], vg_ps[:, :, D:D + E],
                                  t["bg_bc"][:, :].unsqueeze(1).broadcast_to([P, TPB, E]),
                                  ALU.add).then_inc(logits_taken, 1)

            statistics(0, 0, 0)
            scale(0, 0)
            statistics(1, 0, 1)
            scale(1, 1)
            statistics(2, 1, 0)
            scale(2, 0)
            statistics(3, 1, 1)
            dve.wait_ge(now_in, 16 * len(now))
            with dve.Fori(0, (NBLK - 4) // 2) as i:
                for k in range(2):
                    turn = i * 2 + 1 + k
                    take(turn - 1)
                    scale(turn + 2, 1 - k)
                    statistics(turn + 3, i + 2, k)
            dve.wait_ge(later_in, 16 * len(later))
            dve.tensor_tensor(t["shift_bc"][:, :], t["shift_bc"][:, :], bo_bc[:, :], ALU.add)
            dve.tensor_scalar(t["bqs_col"][:, :], t["bq_col"][:, :], SCALE, None, ALU.mult)
            take(NBLK - 4)
            scale(NBLK - 1, 1)
            for blk in range(NBLK - 3, NBLK):
                take(blk)

        @block.gpsimd
        def _(pool):
            pool.memset(t["ident"][:, :], 0.0).then_inc(cleared, 1)
            pool.memset(t["minus_half"][:, :], -0.5).then_inc(cleared, 1)
            pool.wait_ge(cleared, 2)
            pool.affine_select(out=t["ident"][:, :], in_=t["ident"][:, :], compare_op=ALU.not_equal,
                               fill=1.0, base=0, pattern=[[-1, P]], channel_multiplier=1).then_inc(ident_made, 1)
            pool.sem_inc(rstd_done, 2)
            with pool.Fori(0, NBLK // 2) as i:
                for u in range(2):
                    blk = i * 2 + u
                    wait_apart(pool, mv_done, blk + 1, t["passed"][2])
                    pool.tensor_scalar(var[u][:, :], mv[u][:, :, 1], EPS_LN, None, ALU.add).then_inc(pool_chain, 1)
                    pool.tensor_copy(stats[:, ds(blk * TPB, TPB), 0], mv[u][:, :, 0])
                    pool.wait_ge(pool_chain, blk + 1)
                    pool.tensor_tensor(rstd[u][:, :], var[u][:, :], t["minus_half"][:, :], ALU.pow).then_inc(rstd_done, 1)
                    pool.wait_ge(rstd_done, blk + 3)
                    pool.tensor_copy(stats[:, ds(blk * TPB, TPB), 1], rstd[u][:, :])
            pool.wait_ge(later_in, 16 * len(later))
            chain = Chain(pool, b2_chain)
            chain(pool.tensor_copy(b2_parts[:, 0, :], b2_sb[:, :]))
            chain(pool.tensor_tensor(b2_left[:, :], b2_sb[:, :], b2_parts[:, 0, :], ALU.subtract))
            chain(pool.tensor_copy(b2_parts[:, 1, :], b2_left[:, :]))
            pool.tensor_tensor(b2_parts[:, 2, :], b2_left[:, :], b2_parts[:, 1, :], ALU.subtract).then_inc(b2_split, 1)

        @block.scalar
        def _(act):
            for loads, landed in ((now, now_in), (later, later_in)):
                for dst, src in loads:
                    act.dma_start(dst, src).then_inc(landed, 16)
            act.wait_ge(ident_made, 1)
            act.activation(t["warm"][:, :], t["ident"][:, 0:1], ACT.Copy)
            act.sem_inc(ps_freed, 2)
            with act.Fori(0, NBLK // 2) as i:
                for u in range(2):
                    blk = i * 2 + u
                    for c in range(KC):
                        act.wait_ge(transposed, blk * 2 + c + 3)
                        if c == 0:
                            act.wait_ge(projected, blk * TPB + 1)
                        act.activation(xT[u][:, c, :], xT_ps[c][:, :], ACT.Copy).then_inc(xT_copied, 1)
                        act.activation(tok_all[:, ds(blk, 1), c * BLK:(c + 1) * BLK].rearrange("p n s -> p (n s)"),
                                       xT_ps[c][:, :], ACT.Copy).then_inc(ps_freed, 1)

        @block.tensor
        def _(pe):
            pe.sem_inc(transposed, 2)
            pe.sem_inc(projected, 2 * TPB)

            def transpose(blk, u):
                pe.wait_ge(xn_done, blk + 3)
                for c in range(KC):
                    pe.wait_ge(ps_freed, blk * 2 + c + 1)
                    for k in range(TPB):
                        ins = pe.transpose(xT_ps[c][:, k * P:(k + 1) * P], xn[u][:, k, c * P:(c + 1) * P], t["ident"][:, :])
                    ins.then_inc(transposed, 1)

            def project_tokens(blk, u):
                pe.wait_ge(xT_copied, blk * 2 + 2)
                for k in range(TPB):
                    pe.wait_ge(taken, blk * TPB + k + 1)
                    if k == 0:
                        pe.wait_ge(logits_taken, blk + 1)
                    for c in range(KC):
                        ins = pe.matmul(vg_ps[:, k, 0:D + E], xT[u][:, c, k * P:(k + 1) * P], t["wvg_sb"][:, c, :],
                                        start=(c == 0), stop=(c == KC - 1))
                    ins.then_inc(projected, 1)

            pe.wait_ge(ident_made, 1)
            transpose(0, 0)
            pe.wait_ge(now_in, 16 * len(now))
            with pe.Fori(0, NBLK // 2 - 1) as i:
                for k in range(2):
                    transpose(i * 2 + k + 1, 1 - k)
                    project_tokens(i * 2 + k, k)
            transpose(NBLK - 1, 1)
            project_tokens(NBLK - 2, 0)
            project_tokens(NBLK - 1, 1)


def project(nc, sem, sb, ps, t):
    M = 2 * KC
    f32s = [sb(f"f32s{m}", [P, BLK]) for m in range(M)]
    rest = [sb(f"rest{m}", [P, BLK]) for m in range(M)]
    parts = [sb(f"parts{m}", [P, PARTS, BLK], BF16) for m in range(M)]
    qk_ps = [ps(f"qk_ps{m}", [P, BLK]) for m in range(M)]
    route_ps = ps("route_ps", [B * E, S])
    weights = [t["wqT_sb"], t["wqT_sb"], t["wkT_sb"], t["wkT_sb"]]
    biases = [t["bqs_col"], t["bqs_col"], t["bk_col"], t["bk_col"]]
    scales = [SCALE, SCALE, 1.0, 1.0]
    targets = [t["q_parts"], t["q_parts"], t["k_parts"], t["k_parts"]]

    scored = sem("p_scored")
    first = sem("p_first")
    rest_done = sem("p_rest")
    second = sem("p_second")
    third = sem("p_third")
    rest_last, third_last = sem("p_rest_last"), sem("p_third_last")
    stored = [sem(f"p_stored{m}") for m in range(M)]
    shifted, exped = sem("p_shifted"), sem("p_exped")
    routed, route_t = sem("p_routed"), sem("p_route_t")
    masked, mask_stored = sem("p_masked"), sem("p_mask_stored")
    chain = sem("p_chain")
    loop_chain = sem("p_loop_chain")

    lg = t["logits"]
    work = sb("work", [P, 4, TILES, E])
    ex, tmp, hot, hot2 = (work[:, k] for k in range(4))
    red = sb("red", [P, TILES])
    order_i = sb("order_i", [P, E], I32)
    order = sb("order", [P, E])
    denom = sb("denom", [P, ST, E])
    gt = sb("gt", [B * E, S])
    junk = gt[:, 0:S // 2].bitcast(BF16)
    upper = work[0:B * E, 0].rearrange("p n e -> p (n e)").bitcast(BF16)
    eq, cum = (work[0:B * E, 2 * k:2 * k + 2].rearrange("p k n e -> p (k n e)") for k in range(2))
    mask16 = cum[:, 0:S // 2].bitcast(BF16)
    TOP = 30
    power = sb("power", [B * E, TOP + 1])
    bits = sb("bits", [B * E, TOP + 1], I32)
    power_i = sb("power_i", [B * E, TOP + 1], I32)
    cand = sb("cand", [B * E, 1], I32)
    drop = sb("drop", [B * E, 1], I32)
    count = sb("count", [B * E, 1])
    need = sb("need", [B * E, 1])
    ordered = sem("p_ordered")

    with nc.Block() as block:
        @block.tensor
        def _(pe):
            def chunks(lo, hi):
                with pe.Fori(lo, hi) as blk:
                    for m in range(M):
                        pe.wait_ge(first, blk * M + m + 1)
                        for c in range(KC):
                            half = m % KC
                            ins = pe.matmul(qk_ps[m][:, :], weights[m][:, c, half * P:(half + 1) * P],
                                            t["tok_all"][:, ds(blk, 1), c * BLK:(c + 1) * BLK].rearrange("p n s -> p (n s)"),
                                            start=(c == 0), stop=(c == KC - 1))
                        ins.then_inc(scored, 1)

            chunks(0, NBLK // 4)
            pe.wait_ge(routed, 1)
            for s in range(ST):
                ins = pe.transpose(route_ps[:, s * P:(s + 1) * P], tmp[:, s * B:(s + 1) * B, :].rearrange("p b e -> p (b e)"),
                                   t["ident"][:, :])
            ins.then_inc(route_t, 1)
            chunks(NBLK // 4, NBLK)

        @block.scalar
        def _(act):
            act.sem_inc(first, M)
            act.wait_ge(shifted, 1)
            act.activation(ex[:, :, :], lg[:, :, :], ACT.Exp).then_inc(exped, 1)

            def take_first(n, m, blk):
                act.wait_ge(scored, n + 1)
                act.wait_ge(rest_done, n + 1)
                act.activation(f32s[m][:, :], qk_ps[m][:, :], ACT.Identity, bias=biases[m][:, m % KC:m % KC + 1], scale=scales[m])
                act.wait_ge(stored[m], blk * 16 + 16)
                act.activation(parts[m][:, 0, :], qk_ps[m][:, :], ACT.Identity, bias=biases[m][:, m % KC:m % KC + 1],
                               scale=scales[m]).then_inc(first, 1)

            def take_second(n, m):
                act.wait_ge(rest_done, n + 1 + M)
                act.activation(parts[m][:, 1, :], rest[m][:, :], ACT.Copy).then_inc(second, 1)

            take_first(0, 0, 0)
            with act.Fori(0, NBLK - 1) as blk:
                for m in range(M):
                    take_first(blk * M + m + 1, (m + 1) % M, blk + (m + 1) // M)
                    take_second(blk * M + m, m)
            last = (NBLK - 1) * M
            for m in range(M):
                if m + 1 < M:
                    take_first(last + m + 1, m + 1, NBLK - 1)
                act.wait_ge(rest_last, m + 1)
                act.activation(parts[m][:, 1, :], rest[m][:, :], ACT.Copy).then_inc(second, 1)
            act.wait_ge(masked, 1)
            act.dma_start(t["mask_b"], mask16).then_inc(mask_stored, 16)
            act.wait_ge(mask_stored, 16)

        @block.gpsimd
        def _(pool):
            pool.sem_inc(rest_done, M)
            pool.sem_inc(third, M)
            pool.iota(order_i[:, :], pattern=[[-1, E]], base=E, channel_multiplier=0)
            pool.iota(power_i[:, :], pattern=[[-1, TOP + 1]], base=127 + TOP, channel_multiplier=0).then_inc(ordered, 1)

            def take_rest(n, m):
                pool.wait_ge(first, n + 1 + M)
                pool.wait_ge(third, n + 1)
                pool.tensor_tensor(rest[m][:, :], f32s[m][:, :], parts[m][:, 0, :], ALU.subtract).then_inc(rest_done, 1)

            def take_third(n, m):
                pool.wait_ge(second, n + 1)
                pool.tensor_tensor(parts[m][:, 2, :], rest[m][:, :], parts[m][:, 1, :], ALU.subtract).then_inc(third, 1)

            take_rest(0, 0)
            with pool.Fori(0, NBLK - 2) as blk:
                for m in range(M):
                    take_rest(blk * M + m + 1, (m + 1) % M)
                    take_third(blk * M + m, m)
            last = (NBLK - 2) * M
            for m in range(M):
                if m + 1 < M:
                    take_rest(last + m + 1, m + 1)
                take_third(last + m, m)

        @block.sync
        def _(sp):
            for m in range(M):
                sp.sem_inc(stored[m], 16)
            def store(blk, m):
                row = (blk // BPS) * D + (m % KC) * P
                sp.dma_start(targets[m][:, ds(row, P), ds((blk % BPS) * BLK, BLK)].rearrange("r p s -> p r s"),
                             parts[m][:, :, :]).then_inc(stored[m], 16)

            with sp.Fori(0, NBLK - 1) as blk:
                for m in range(M):
                    sp.wait_ge(third, blk * M + m + 1 + M)
                    store(blk, m)
            for m in range(M):
                sp.wait_ge(third_last, m + 1)
                store(NBLK - 1, m)
            for m in range(M):
                sp.wait_ge(stored[m], 16 * NBLK + 16)

        @block.vector
        def _(dve):
            do = Chain(dve, chain)
            wide = lambda a: a[:, :].unsqueeze(2).broadcast_to([P, TILES, E])
            do(dve.tensor_reduce(red[:, :], lg[:, :, :], AX.X, ALU.max))
            dve.tensor_tensor(lg[:, :, :], lg[:, :, :], wide(red), ALU.subtract).then_inc(shifted, 1)
            dve.wait_ge(exped, 1)
            do(dve.tensor_reduce(red[:, :], ex[:, :, :], AX.X, ALU.add))
            do(dve.reciprocal(red[:, :], red[:, :]))
            do(dve.tensor_tensor(ex[:, :, :], ex[:, :, :], wide(red), ALU.mult))
            dve.wait_ge(ordered, 1)
            do(dve.tensor_copy(order[:, :], order_i[:, :]))
            do(dve.tensor_scalar(power[:, :].bitcast(I32), power_i[:, :], 23, None, ALU.logical_shift_left))
            do(dve.tensor_copy(bits[:, :], power[:, :]))
            order_bc = order[:, :].unsqueeze(1).broadcast_to([P, TILES, E])
            scores = ex
            for k, h in enumerate((hot, hot2)):
                do(dve.tensor_reduce(red[:, :], scores[:, :, :], AX.X, ALU.max))
                do(dve.tensor_tensor(h[:, :, :], scores[:, :, :], wide(red), ALU.is_equal))
                do(dve.tensor_tensor(h[:, :, :], h[:, :, :], order_bc, ALU.mult))
                do(dve.tensor_reduce(red[:, :], h[:, :, :], AX.X, ALU.max))
                do(dve.tensor_tensor(h[:, :, :], h[:, :, :], wide(red), ALU.is_equal))
                if k == 0:
                    do(dve.scalar_tensor_tensor(tmp[:, :, :], hot[:, :, :], -4.0, ex[:, :, :], ALU.mult, ALU.add))
                    scores = tmp
            do(dve.tensor_tensor(hot[:, :, :], hot[:, :, :], hot2[:, :, :], ALU.add))
            do(dve.tensor_tensor(ex[:, :, :], ex[:, :, :], hot[:, :, :], ALU.mult))
            by_batch = ex[:, :, :].rearrange("p (b s) e -> p b s e", b=B)
            do(dve.tensor_tensor(denom[:, :, :], by_batch[:, 0], by_batch[:, 1], ALU.add))
            for b in range(2, B):
                do(dve.tensor_tensor(denom[:, :, :], denom[:, :, :], by_batch[:, b], ALU.add))
            do(dve.tensor_scalar(denom[:, :, :], denom[:, :, :], EPS_GATE, None, ALU.add))
            do(dve.reciprocal(denom[:, :, :], denom[:, :, :]))
            routes = tmp[:, :, :].rearrange("p (s b) e -> p b s e", b=B)
            for b in range(B):
                do(dve.scalar_tensor_tensor(routes[:, b], by_batch[:, b], float(B), denom[:, :, :], ALU.mult, ALU.mult))
            dve.memset(cand[:, :], 1 << TOP).then_inc(routed, 1)
            dve.wait_ge(route_t, 1)
            do(dve.tensor_copy(upper, route_ps[:, :].bitcast(BF16).rearrange("p (n two) -> p n two", two=2)[:, :, 1]))

            def try_bit(step, k, weights, last=False):
                step(dve.tensor_scalar(junk, weights, cand[:, :].bitcast(F32), None, ALU.is_ge, ALU.add,
                                       accum_out=count[:, :]))
                step(dve.tensor_scalar(drop[:, :], count[:, :], TOPK_TOKENS - 0.5, power[:, ds(k, 1)], ALU.is_lt, ALU.mult))
                if last:
                    step(dve.tensor_tensor(cand[:, :], cand[:, :], drop[:, :], ALU.bitwise_xor))
                else:
                    step(dve.scalar_tensor_tensor(cand[:, :], cand[:, :], drop[:, :], bits[:, ds(k + 1, 1)],
                                                  ALU.bitwise_xor, ALU.bitwise_or))

            STEP, UNROLL = 3, 3
            UPPER = TOP - 15
            for begin, weights in ((0, upper), (UPPER, route_ps[:, :])):
                with dve.Fori(begin // UNROLL, (begin + UPPER) // UNROLL) as i:
                    step = Chain(dve, loop_chain, i * (STEP * UNROLL))
                    for j in range(UNROLL):
                        try_bit(step, i * UNROLL + j, weights)
            try_bit(do, TOP, route_ps[:, :], last=True)
            bound = cand[:, :].bitcast(F32)
            do(dve.tensor_scalar(gt[:, :], route_ps[:, :], bound, None, ALU.is_gt, ALU.add, accum_out=count[:, :]))
            do(dve.tensor_scalar(need[:, :], count[:, :], -1.0, float(TOPK_TOKENS), ALU.mult, ALU.add))
            do(dve.tensor_scalar(eq[:, :], route_ps[:, :], bound, None, ALU.is_equal))
            do(dve.tensor_tensor_scan(cum[:, :], eq[:, :], eq[:, :], 0.0, ALU.add, ALU.max))
            do(dve.scalar_tensor_tensor(eq[:, :], cum[:, :], need[:, :], eq[:, :], ALU.is_le, ALU.mult))
            do(dve.tensor_tensor(gt[:, :], gt[:, :], eq[:, :], ALU.add))
            dve.tensor_copy(mask16, gt[:, :]).then_inc(masked, 1)

            last = (NBLK - 1) * M

            def last_third(m):
                dve.wait_ge(second, last + m + 1)
                dve.tensor_tensor(parts[m][:, 2, :], rest[m][:, :], parts[m][:, 1, :], ALU.subtract).then_inc(third_last, 1)

            for m in range(M):
                dve.wait_ge(first, last + m + 1 + M)
                dve.wait_ge(third, last + m + 1)
                dve.tensor_tensor(rest[m][:, :], f32s[m][:, :], parts[m][:, 0, :], ALU.subtract).then_inc(rest_last, 1)
                if m:
                    last_third(m - 1)
            last_third(M - 1)


def experts(nc, sem, sb, ps, t):
    QTR = EP // 4
    w1_hi = sb("w1_hi", [P, KC, E * F], F32R)
    w1_lo = sb("w1_lo", [P, KC, E * F], F32R)
    w2_hi = sb("w2_hi", [P, EP, D], F32R)
    w2_lo = sb("w2_lo", [P, EP, D], F32R)
    mask_bc = [sb(f"mask_bc{q}", [P, QTR, BLK], BF16) for q in range(2)]
    mask_rows = sb("mask_rows", [PARTS * E, BLK], BF16)
    x_in = sb("xe_in", [P, TPB, D])
    z = sb("z", [P, TPB, D])
    xn_hi = [sb(f"xn_hi{u}", [P, KC * BLK], F32R) for u in range(2)]
    xn_lo = [sb(f"xn_lo{u}", [P, KC * BLK], F32R) for u in range(2)]
    g = [sb(f"g{r}", [P, BLK]) for r in range(2)]
    g_hi = [sb(f"g_hi{r}", [P, BLK], F32R) for r in range(2)]
    g_lo = [sb(f"g_lo{r}", [P, BLK], F32R) for r in range(2)]
    bn = sb("bn_z", [P, TPB, 6])
    mv = sb("mv_z", [P, TPB, 2])
    var = sb("var_z", [P, TPB])
    rstd = sb("rstd_z", [P, TPB])
    h_ps = [ps(f"h_ps{r}", [P, BLK]) for r in range(2)]
    o_ps = [ps(f"o_ps{k}", [P, BLK])[:, 0:D] for k in range(TPB)]
    tok_all, stats = t["tok_all"], t["stats_all"]
    AHEAD = 2

    def xn(blk):
        return tok_all[:, ds(blk, 1), :].rearrange("p n s -> p (n s)")

    flat = lambda a: a[:, :, :].rearrange("p k d -> p (k d)")
    w1_cols = [slice(q * 2 * P, (q + 1) * 2 * P) for q in range(4)]
    w1_raw = [a[:, k:k + KC, :] for a in (z, x_in) for k in range(0, TPB, KC)]
    pieces = [*([(w1_raw[q], w1_hi[:, :, w1_cols[q]], w1_lo[:, :, w1_cols[q]])] for q in range(4)),
              [(g[k][:, :], *(flat(w)[:, k * BLK:(k + 1) * BLK] for w in (w2_hi, w2_lo))) for k in range(2)],
              [(flat(z), *(flat(w)[:, 2 * BLK:4 * BLK] for w in (w2_hi, w2_lo)))]]
    piece_in = [sem(f"e_piece_in{k}") for k in range(len(pieces))]
    piece_rounded, piece_split = sem("e_piece_rounded"), sem("e_piece_split")
    masks_in = [sem(f"e_masks_in{q}") for q in range(2)]
    loaded = sem("e_loaded")
    xn_rounded, xn_split = sem("e_xn_rounded"), sem("e_xn_split")
    hidden = sem("e_hidden")
    gelu = sem("e_gelu")
    gated = sem("e_gated")
    rounded = sem("e_rounded")
    split = sem("e_split")
    used = sem("e_used")
    summed = sem("e_summed")
    z_done = sem("e_z")
    bn_done, mv_done, rstd_done, pool_chain = sem("e_bn"), sem("e_mv"), sem("e_rstd"), sem("e_pool")
    normed = sem("e_normed")
    renormed = sem("e_renormed")
    shifted = sem("e_shifted")
    scaled = sem("e_scaled")
    based = sem("e_based")

    with nc.Block() as block:
        @block.sync
        def _(sp):
            def masks(blk, q):
                for k in range(2):
                    src = t["mask_b"].rearrange("(b e k) s -> b k e s", b=B, k=2)[
                        ds(blk // BPS, 1), k, q * QTR:(q + 1) * QTR, ds((blk % BPS) * BLK, BLK)]
                    sp.dma_start(mask_bc[q % 2][k * F:(k + 1) * F, :, :],
                                 src.broadcast_to([F, QTR, BLK])).then_inc(masks_in[q % 2], 16)

            def tokens(blk):
                src = t["mask_b"][ds((blk // BPS) * E, E), ds((blk % BPS) * BLK, BLK)]
                sp.dma_start(mask_rows[:, :], src.unsqueeze(0).broadcast_to([PARTS, E, BLK])).then_inc(loaded, 16)
                sp.dma_start(x_in[:, :, :], t["x_blocks"][ds(blk, 1)].rearrange("n p t d -> (n p) t d")).then_inc(loaded, 16)

            w1_rows = t["w1"].rearrange("(c p) n -> p c n", p=P)
            w2_rows = t["w2"].rearrange("(c p) n -> p c n", p=P)
            for q in range(4):
                sp.dma_start(w1_raw[q], w1_rows[:, :, w1_cols[q]]).then_inc(piece_in[q], 16)
            for k in range(2):
                sp.dma_start(g[k][:, :].rearrange("p (c n) -> p c n", c=2), w2_rows[:, 2 * k:2 * k + 2, :]).then_inc(piece_in[4], 16)
            masks(0, 0)
            sp.wait_ge(piece_split, 2)
            sp.dma_start(z[:, :, :], w2_rows[:, 4:8, :]).then_inc(piece_in[5], 16)
            masks(0, 1)
            sp.wait_ge(piece_split, 4)
            tokens(0)

            def step(blk, following=True):
                for q in range(4):
                    if q < 2 or following:
                        sp.wait_ge(gated, blk * EP + (q + 1) * QTR)
                        masks(blk + q // 2, (q + 2) % 4)
                    if q == 1 and not (isinstance(blk, int) and blk == 0):
                        sp.wait_ge(based, blk + 2)
                        tokens(blk)

            step(0)
            with sp.Fori(1, NBLK - 1) as blk:
                step(blk)
            step(NBLK - 1, following=False)

        @block.tensor
        def _(pe):
            pe.sem_inc(used, 2)

            def hide(blk, u, e):
                n = blk * EP + e
                if e == 0:
                    pe.wait_ge(xn_split, blk + 1)
                pe.wait_ge(piece_split, 1 + e // 2)
                pe.wait_ge(gelu, n + 1)
                pair = slice(e * P, (e + 1) * P)
                for c in range(KC):
                    col = slice(c * BLK, (c + 1) * BLK)
                    hi, lo = xn_hi[u][:, col], xn_lo[u][:, col]
                    for k, (w, v) in enumerate(((w1_hi[:, c, pair], hi), (w1_hi[:, c, pair], lo), (w1_lo[:, c, pair], hi))):
                        ins = pe.matmul(h_ps[e % 2][:, :], w, v, start=(c == 0 and k == 0), stop=(c == KC - 1 and k == 2))
                ins.then_inc(hidden, 1)

            def unhide(blk, u, e):
                pe.wait_ge(piece_split, 5 + e // 4)
                pe.wait_ge(split, blk * EP + e + 3)
                for k in range(TPB):
                    if e == 0:
                        pe.wait_ge(z_done, blk * TPB + k + 1)
                    hi, lo = (part[:, k * P:(k + 1) * P] for part in (g_hi[e % 2], g_lo[e % 2]))
                    for m, (v, w) in enumerate(((hi, w2_hi), (hi, w2_lo), (lo, w2_hi))):
                        ins = pe.matmul(o_ps[k], v, w[:, e, :], start=(e == 0 and m == 0), stop=False)
                ins.then_inc(used, 1)

            def block_step(blk, u, following=True):
                for e in range(EP):
                    if e + AHEAD < EP:
                        hide(blk, u, e + AHEAD)
                    elif following:
                        hide(blk + 1, 1 - u, e + AHEAD - EP)
                    unhide(blk, u, e)
                pe.wait_ge(loaded, (blk + 1) * 32)
                for k in range(TPB):
                    pe.matmul(o_ps[k], mask_rows[:, k * P:(k + 1) * P], t["b2_rows"][:, :],
                              start=False, stop=True).then_inc(summed, 1)

            for e in range(AHEAD):
                hide(0, 0, e)
            with pe.Fori(0, NBLK // 2 - 1) as i:
                for u in range(2):
                    block_step(i * 2 + u, u)
            for u in range(2):
                block_step(NBLK - 2 + u, u, following=(u == 0))

        @block.scalar
        def _(act):
            act.activation(t["warm"][:, :], t["ident"][:, 0:1], ACT.Gelu)
            act.sem_inc(gelu, 2)
            act.sem_inc(split, 2)

            def round_xn(blk, u):
                act.activation(xn_hi[u][:, :], xn(blk), ACT.Copy).then_inc(xn_rounded, 1)

            def hidden_units(blk, e):
                n = blk * EP + e
                act.wait_ge(hidden, n + 1)
                act.wait_ge(split, n + 1)
                act.activation(g[e % 2][:, :], h_ps[e % 2][:, :], ACT.Gelu, bias=t["b1_col"][:, e:e + 1]).then_inc(gelu, 1)
                act.wait_ge(gated, n + 1)
                act.wait_ge(used, n + 1)
                act.activation(g_hi[e % 2][:, :], g[e % 2][:, :], ACT.Copy).then_inc(rounded, 1)

            def block_step(blk, u, following=True):
                for e in range(EP):
                    hidden_units(blk, e)
                    if following and e == 1:
                        act.wait_ge(hidden, blk * EP)
                        round_xn(blk + 1, 1 - u)

            round_xn(0, 0)
            for k, piece in enumerate(pieces):
                act.wait_ge(piece_in[k], 16 * len(piece))
                for src, hi, lo in piece:
                    ins = act.activation(hi, src, ACT.Copy)
                ins.then_inc(piece_rounded, 1)
            act.wait_ge(piece_split, 5)
            block_step(0, 0)
            with act.Fori(0, NBLK // 2 - 1) as i:
                for u in range(2):
                    block_step(i * 2 + 1 + u, 1 - u)
            block_step(NBLK - 1, 1, following=False)

        @block.vector
        def _(dve):
            dve.sem_inc(z_done, TPB)

            def gate(blk, e):
                q = e // QTR
                if e % QTR == 0:
                    dve.wait_ge(masks_in[q % 2], (blk * 2 + q // 2 + 1) * 32)
                dve.wait_ge(gelu, blk * EP + e + 3)
                dve.tensor_tensor(g[e % 2][:, :], g[e % 2][:, :], mask_bc[q % 2][:, e % QTR, :], ALU.mult).then_inc(gated, 1)

            def renormalise(blk):
                dve.wait_ge(loaded, (blk + 1) * 32)
                for k in range(TPB):
                    st = stats[:, ds(blk * TPB + k, 1), :].rearrange("p n s -> p (n s)")
                    ins = dve.tensor_scalar(z[:, k, :], x_in[:, k, :], st[:, 0:1], st[:, 1:2], ALU.subtract, ALU.mult)
                ins.then_inc(renormed, 1)
                dve.wait_ge(renormed, blk + 1)
                dve.tensor_tensor(x_in[:, :, :], x_in[:, :, :], t["shift_bc"][:, :].unsqueeze(1).broadcast_to([P, TPB, D]),
                                  ALU.add).then_inc(shifted, 1)

            def add_sum(blk):
                for k in range(TPB):
                    dve.wait_ge(summed, blk * TPB + k + 1)
                    dve.tensor_tensor(z[:, k, :], z[:, k, :], o_ps[k], ALU.add).then_inc(z_done, 1)

            def statistics(blk):
                dve.wait_ge(z_done, blk * TPB + 2 * TPB)
                for k in range(TPB):
                    ins = dve.bn_stats(bn[:, k, :], z[:, k, :])
                ins.then_inc(bn_done, 1)
                wait_apart(dve, bn_done, blk + 1, t["passed"][0])
                for k in range(TPB):
                    ins = dve.bn_aggr(mv[:, k, :], bn[:, k, :])
                ins.then_inc(mv_done, 1)

            def scale(blk):
                dve.wait_ge(rstd_done, blk + 1)
                for k in range(TPB):
                    ins = dve.tensor_scalar(z[:, k, :], z[:, k, :], mv[:, k, 0:1], rstd[:, k:k + 1], ALU.subtract, ALU.mult)
                ins.then_inc(normed, 1)

            def times_gamma(blk):
                dve.wait_ge(normed, blk + 1)
                dve.tensor_tensor(z[:, :, :], z[:, :, :], t["gamma_bc"][:, :].unsqueeze(1).broadcast_to([P, TPB, D]),
                                  ALU.mult).then_inc(scaled, 1)

            def split_xn(blk, u):
                dve.wait_ge(xn_rounded, blk + 1)
                dve.tensor_tensor(xn_lo[u][:, :], xn(blk), xn_hi[u][:, :].bitcast(F32), ALU.subtract).then_inc(xn_split, 1)

            def gates(blk, u, last=True, following=True):
                for e in range(EP):
                    gate(blk, e)
                    if last and e == AHEAD - 1:
                        add_sum(blk - 1)
                        statistics(blk - 1)
                    if last and e == AHEAD:
                        scale(blk - 1)
                    if last and e == AHEAD + 1:
                        times_gamma(blk - 1)
                    if following and e == AHEAD + 2:
                        split_xn(blk + 1, 1 - u)
                    if e == EP - 1:
                        renormalise(blk)

            split_xn(0, 0)
            for k, piece in enumerate(pieces):
                dve.wait_ge(piece_rounded, k + 1)
                for src, hi, lo in piece:
                    ins = dve.tensor_tensor(lo, src, hi.bitcast(F32), ALU.subtract)
                ins.then_inc(piece_split, 1)
            dve.wait_ge(piece_split, 6)
            gates(0, 0, last=False)
            with dve.Fori(0, NBLK // 2 - 1) as i:
                for u in range(2):
                    gates(i * 2 + 1 + u, 1 - u)
            gates(NBLK - 1, 1, following=False)
            add_sum(NBLK - 1)
            statistics(NBLK - 1)
            scale(NBLK - 1)
            times_gamma(NBLK - 1)

        @block.gpsimd
        def _(pool):
            pool.sem_inc(based, 2)

            def split_units(blk, e):
                n = blk * EP + e
                pool.wait_ge(rounded, n + 1)
                pool.tensor_tensor(g_lo[e % 2][:, :], g[e % 2][:, :], g_hi[e % 2][:, :].bitcast(F32), ALU.subtract).then_inc(split, 1)

            def invert(blk):
                chain = Chain(pool, pool_chain, blk)
                wait_apart(pool, mv_done, blk + 1, t["passed"][2])
                chain(pool.tensor_scalar(var[:, :], mv[:, :, 1], EPS_LN, None, ALU.add))
                pool.tensor_tensor(rstd[:, :], var[:, :], t["minus_half"][:, :], ALU.pow).then_inc(rstd_done, 1)

            def finish(blk):
                pool.wait_ge(shifted, blk + 1)
                pool.wait_ge(scaled, blk + 1)
                pool.tensor_tensor(tok_all[:, ds(blk, 1), :].rearrange("p n (k d) -> p (n k) d", k=TPB),
                                   z[:, :, :], x_in[:, :, :], ALU.add).then_inc(based, 1)

            def block_step(blk, last=True):
                for e in range(EP):
                    split_units(blk, e)
                    if last and e == AHEAD - 1:
                        invert(blk - 1)
                    if last and e == AHEAD + 1:
                        finish(blk - 1)

            block_step(0, last=False)
            with pool.Fori(1, NBLK) as blk:
                block_step(blk)
            invert(NBLK - 1)
            finish(NBLK - 1)


def attend(nc, sem, sb, ps, t):
    R = 3
    q_feat = [sb(f"q_feat{r}", [FEAT + SHIFT, S], BF16) for r in range(R)]
    k_feat = [sb(f"k_feat{r}", [FEAT + SHIFT, S], BF16) for r in range(R)]
    prob = [sb(f"prob{r}", [P, S]) for r in range(R)]
    v_head = [sb(f"v_head{r}", [P, ST, VW]) for r in range(R)]
    att = [sb(f"att{r}", [P, BLK]) for r in range(R)]
    half_max = [sb(f"half_max{r}", [P, ST, 2]) for r in range(R)]
    row_max = [sb(f"row_max{r}", [P, ST]) for r in range(R)]
    left = sb("left", [P, ST])
    minus_one = sb("minus_one", [P, ST])
    shift = sb("shift", [P, SHIFT, ST], BF16)
    shift_t = sb("shift_t", [SHIFT * ST, P], BF16)
    ident16 = sb("ident16", [P, P], BF16)
    s_ps = [ps(f"s_ps{r}", [P, BLK]) for r in range(R)]
    m_ps = [ps(f"m_ps{r}", [P, 2 * BLK]) for r in range(2)]
    a_ps = ps("a_ps", [P, BLK])
    QB = S // BLK
    PAIRS = ST * 2
    shift_ps = m_ps[0][:, :].bitcast(BF16)[0:SHIFT * ST, 0:P]

    fed = [sem(f"a_fed{r}") for r in range(R)]
    LOADS = len(Q_ORDER) + len(K_ORDER)
    piece = sem("a_piece")
    maxed = sem("a_maxed")
    row_maxed = sem("a_row_maxed")
    shift_done = sem("a_shift")
    shift_turned = sem("a_turned")
    shift_read = sem("a_shift_read")
    shift_in = sem("a_shift_in")
    scored = sem("a_scored")
    exped = sem("a_exped")
    weighed = sem("a_weighed")
    v_ready = sem("a_v_ready")
    att_read = sem("a_att_read")
    att_out = [sem(f"a_att_out{r}") for r in range(R)]
    chain_sem = sem("a_chain")
    sums_in, sums_inverted, sem_inv_chain = sem("a_sums_in"), sem("a_sums_inverted"), sem("a_inv_chain")
    sums = sb("sums", [P, BLK])
    spread_f, spread_chain = sb("spread_f", [H * PARTS, D]), sem("a_spread")
    consts, consts16, ones_made = sem("a_consts"), sem("a_consts16"), sem("a_ones_made")

    PER = 2
    EARLY = 5 * PER
    AFTER = ST - 4
    assert EARLY + (AFTER - 1) * PER == PAIRS
    TURN_AT = AFTER + 2
    TURN_PIECE = (TURN_AT - AFTER) * PER
    LINKS = 4

    with nc.Block() as block:
        @block.gpsimd
        def _(pool):
            for r in range(R):
                pool.memset(v_head[r][:, :, :], 1.0)
            pool.memset(minus_one[:, :], -1.0).then_inc(consts, 1)
            pool.wait_ge(consts, 1)

            def copy_v(n, r):
                pool.tensor_copy(v_head[r][:, :, 0:HD],
                                 t["v_all"][:, :, :, :, :].rearrange("p b h s d -> p (b h) s d")[:, ds(n, 1)].rearrange("p n s d -> p (n s) d")
                                 ).then_inc(v_ready, 1)

            def split_shift(n, r):
                pool.wait_ge(row_maxed, n + 1)
                if not (isinstance(n, int) and n == 0):
                    pool.wait_ge(shift_turned, n)
                do = Chain(pool, chain_sem, n * LINKS)
                do(pool.tensor_tensor(shift[:, 0, :], row_max[r][:, :], minus_one[:, :], ALU.mult))
                do(pool.tensor_tensor(left[:, :], row_max[r][:, :], shift[:, 0, :], ALU.add))
                do(pool.tensor_tensor(shift[:, 1, :], left[:, :], minus_one[:, :], ALU.mult))
                do(pool.tensor_tensor(left[:, :], left[:, :], shift[:, 1, :], ALU.add))
                pool.tensor_tensor(shift[:, 2, :], left[:, :], minus_one[:, :], ALU.mult).then_inc(shift_done, 1)

            pool.memset(spread_f[:, :], 1.0).then_inc(spread_chain, 1)
            pool.wait_ge(spread_chain, 1)
            pool.affine_select(out=spread_f[:, :], in_=spread_f[:, :], compare_op=ALU.is_ge, fill=0.0, base=0,
                               pattern=[[-PARTS, H], [0, HD]], channel_multiplier=1).then_inc(spread_chain, 1)
            pool.wait_ge(spread_chain, 2)
            pool.affine_select(out=spread_f[:, :], in_=spread_f[:, :], compare_op=ALU.is_ge, fill=0.0, base=PARTS - 1,
                               pattern=[[PARTS, H], [0, HD]], channel_multiplier=-1).then_inc(spread_chain, 1)
            pool.wait_ge(spread_chain, 3)
            pool.tensor_copy(t["spread"][:, :], spread_f[:, :]).then_inc(spread_chain, 1)
            pool.wait_ge(spread_chain, 4)
            for r in range(R):
                pool.memset(k_feat[r][FEAT:FEAT + SHIFT, :], 1.0).then_inc(ones_made, 1)
            pool.wait_ge(ones_made, R)
            for n in range(R):
                copy_v(n, n)
            split_shift(0, 0)
            with pool.Fori(0, (HEADS - R - 1) // R) as i:
                for r in range(R):
                    n = i * R + R + r
                    split_shift(n - R + 1, (r + 1) % R)
                    pool.wait_ge(weighed, (n - R + 1) * ST + 3)
                    copy_v(n, r)
            for n in range(HEADS - 1, HEADS + R - 1):
                split_shift(n - R + 1, (n + 1) % R)
                if n < HEADS:
                    pool.wait_ge(weighed, (n - R + 1) * ST + 3)
                    copy_v(n, n % R)

        @block.sync
        def _(sp):
            def feed(n, r):
                for parts, feat, order in ((t["q_parts"], q_feat[r], Q_ORDER), (t["k_parts"], k_feat[r], K_ORDER)):
                    at = 0
                    for first, count in order:
                        rows = parts[:, ds(n * HD, HD), :]
                        if parts is t["q_parts"]:
                            src = rows[first:first + 1].broadcast_to([count, HD, S])
                        else:
                            src = rows[first:first + count]
                        sp.dma_start(feat[at:at + count * HD, :], src).then_inc(fed[r], 16)
                        at += count * HD

            def put_shift(n, r):
                sp.wait_ge(shift_read, n + 1)
                sp.dma_start(q_feat[r][FEAT:FEAT + SHIFT, :].rearrange("k (q p) -> k q p", p=P),
                             shift_t[:, :]).then_inc(shift_in, 16)

            def put_att(g, r):
                sp.wait_ge(att_read, g + 2)
                sp.dma_start(t["att_dram"][ds(g, 1)].rearrange("n p s -> (n p) s"), att[r][:, :]).then_inc(att_out[r], 16)

            for r in range(R):
                sp.sem_inc(att_out[r], 16)
            for n in range(R):
                feed(n, n)
            put_shift(0, 0)
            def step(g, r, more=True):
                put_shift(g + 1, (r + 1) % R)
                if more:
                    sp.wait_ge(scored, (g + 1) * ST * QB)
                    feed(g + R, r)
                put_att(g, r)

            with sp.Fori(0, (HEADS - R - 1) // R) as i:
                for r in range(R):
                    step(i * R + r, r)
            for g in range(HEADS - R - 1, HEADS - 1):
                step(g, g % R, g + R < HEADS)
                if g == HEADS - R:
                    for r in range(R):
                        sp.wait_ge(att_out[r], 16 * (HEADS // 2 // R + 2))
                    sp.dma_start(sums[:, :], sum_rows(t, 0)).then_inc(sums_in, 16)
                if g == HEADS - 2:
                    sp.wait_ge(sums_inverted, 1)
                    sp.dma_start(t["inverse_dram"][0:P], t["inv_parts"][:, :, :]).then_inc(sums_in, 16)
            sp.dma_start(t["woT_sb"][:, :, :], t["woT"].rearrange("(c p) n -> p c n", p=P)).then_inc(t["out_loaded"][0], 16)
            sp.wait_ge(sums_in, 32)
            load_block(sp, t, 0, 0)
            put_att(HEADS - 1, (HEADS - 1) % R)
            for r in range(R):
                sp.wait_ge(att_out[r], 16 * (len(range(r, HEADS, R)) + 1))

        @block.scalar
        def _(act):
            act.sem_inc(exped, R)
            act.sem_inc(att_read, 1)

            def exps(g, it, r, kt, shift_of=None):
                for qb in range(QB):
                    n = (g * ST + kt) * QB + qb
                    c = (r * ST + kt) * QB + qb
                    if kt == TURN_AT - 1 and qb == QB - 1 and shift_of is not None:
                        read_shift(shift_of)
                    if qb == 0:
                        act.wait_ge(weighed, g * ST + kt + 1)
                    act.wait_ge(scored, n + 1)
                    act.activation(prob[(c // QB) % R][:, qb * BLK:(qb + 1) * BLK], s_ps[c % R][:, :], ACT.Exp).then_inc(exped, 1)

            def read_shift(n):
                act.wait_ge(shift_turned, n + 1)
                act.activation(shift_t[:, :], shift_ps, ACT.Copy).then_inc(shift_read, 1)

            def collect(g, it, r):
                act.wait_ge(weighed, (g + 1) * ST + 3)
                act.wait_ge(att_out[r], it * 16 + 16)
                act.activation(att[r][:, :], a_ps[:, :], ACT.Copy).then_inc(att_read, 1)

            read_shift(0)
            exps(0, 0, 0, 0)
            with act.Fori(0, HEADS // R) as i:
                for r in range(R):
                    g = i * R + r
                    for kt in range(1, ST):
                        exps(g, i, r, kt, g + 1)
                    exps(g + 1, i + (r + 1) // R, (r + 1) % R, 0)
                    collect(g, i, r)
            g = HEADS - 1
            for kt in range(1, ST):
                exps(g, g // R, g % R, kt)
            collect(g, g // R, g % R)

        @block.tensor
        def _(pe):
            pe.sem_inc(weighed, R)

            def pass1(n, r, p, shift_before=True):
                pe.wait_ge(maxed, n * PAIRS + p + 1)
                if p == TURN_PIECE and shift_before:
                    pe.wait_ge(shift_read, n)
                qt, half = divmod(p, 2)
                for k in range(2):
                    key = half * 2 * BLK + k * BLK
                    ins = pe.matmul(m_ps[p % 2][:, k * BLK:(k + 1) * BLK], q_feat[r][0:FEAT, qt * P:(qt + 1) * P],
                                    k_feat[r][0:FEAT, key:key + BLK], start=True, stop=True)
                ins.then_inc(piece, 1)

            def turn(n, more=True):
                if more:
                    pe.wait_ge(maxed, (n + 1) * PAIRS + TURN_PIECE - 1 + 2)
                wait_apart(pe, shift_done, n + 1, t["passed"][1])
                pe.transpose(shift_ps, shift[:, :, :].rearrange("p k q -> p (k q)"), ident16[:, :]).then_inc(shift_turned, 1)

            def score(g, r, kt, qb):
                n = (g * ST + kt) * QB + qb
                c = (r * ST + kt) * QB + qb
                pe.wait_ge(exped, n + 1)
                pe.matmul(s_ps[c % R][:, :], k_feat[r][:, kt * P:(kt + 1) * P], q_feat[r][:, qb * BLK:(qb + 1) * BLK],
                          start=True, stop=True).then_inc(scored, 1)

            def weigh(g, r, kt):
                if kt == 0:
                    pe.wait_ge(v_ready, g + 1)
                    pe.wait_ge(att_read, g + 1)
                pe.wait_ge(exped, (g * ST + kt) * QB + QB + R)
                for qb in range(QB):
                    ins = pe.matmul(a_ps[qb * VW:(qb + 1) * VW, :], v_head[r][:, kt, :],
                                    prob[(r * ST + kt) % R][:, qb * BLK:(qb + 1) * BLK],
                                    start=(kt == 0), stop=(kt == ST - 1))
                ins.then_inc(weighed, 1)

            def wait_fed(r, it):
                pe.wait_ge(fed[r % R], (it + r // R + 1) * 16 * LOADS)

            def key_tile(g, r, kt, last, pieces, between=lambda: None):
                score(g, r, kt, 0)
                for qb, p in enumerate(pieces):
                    pass1(*p)
                    score(g, r, kt, qb + 1)
                if not pieces:
                    score(g, r, kt, 1)
                    score(g, r, kt, 2)
                if last is not None:
                    weigh(*last)
                between()
                score(g, r, kt, 3)

            def step(g, r, it, following=True, after=True):
                nr, ar = (r + 1) % R, (r + 2) % R
                for kt in range(1, AFTER):
                    p = EARLY + (kt - 1) * PER
                    pieces = [(g + 1, nr, p + k) for k in range(PER)] if following else []
                    key_tile(g, r, kt, (g, r, kt - 1), pieces)
                if after:
                    wait_fed(r + 2, it)
                early = [[(g + 2, ar, j * PER + k) for k in range(PER)] if after else [] for j in range(EARLY // PER)]
                for j, kt in enumerate(range(AFTER, ST)):
                    turns = following and kt == TURN_AT - 1
                    key_tile(g, r, kt, (g, r, kt - 1), early[j],
                             **({"between": lambda: turn(g + 1, after)} if turns else {}))
                if following:
                    pe.wait_ge(shift_in, (g + 2) * 16)
                    key_tile(g + 1, nr, 0, (g, r, ST - 1), early[-1])
                else:
                    weigh(g, r, ST - 1)

            pe.wait_ge(consts16, 1)
            wait_fed(0, 0)
            for p in range(PAIRS):
                pass1(0, 0, p, shift_before=False)
            wait_fed(1, 0)
            for p in range(EARLY - PER):
                if p == TURN_PIECE:
                    turn(0)
                pass1(1, 1, p)
            pe.wait_ge(shift_in, 16)
            pe.wait_ge(ones_made, R)
            key_tile(0, 0, 0, None, [(1, 1, EARLY - PER + k) for k in range(PER)])
            rounds = (HEADS - 2) // R
            with pe.Fori(0, rounds) as i:
                for r in range(R):
                    step(i * R + r, r, i)
            for g in range(rounds * R, HEADS):
                step(g, g % R, g // R, following=g + 1 < HEADS, after=g + 2 < HEADS)

        @block.vector
        def _(dve):
            dve.tensor_copy(ident16[:, :], t["ident"][:, :]).then_inc(consts16, 1)
            dve.sem_inc(maxed, 2)

            def maxima(n, r):
                for p in range(PAIRS):
                    dve.wait_ge(piece, n * PAIRS + p + 1)
                    if p == 0 and not (isinstance(n, int) and n < R):
                        dve.wait_ge(shift_done, n - R + 1)
                    dve.tensor_reduce(half_max[r][:, p // 2, p % 2:p % 2 + 1], m_ps[p % 2][:, :], AX.X, ALU.max).then_inc(maxed, 1)
                dve.wait_ge(maxed, n * PAIRS + PAIRS + 2)
                dve.tensor_reduce(row_max[r][:, :], half_max[r][:, :, :], AX.X, ALU.max).then_inc(row_maxed, 1)

            for n in range(R):
                maxima(n, n)
            with dve.Fori(1, HEADS // R) as i:
                for r in range(R):
                    maxima(i * R + r, r)
            maxima(HEADS - 1, (HEADS - 1) % R)
            dve.wait_ge(sums_in, 16)
            invert_sums(dve, t, sums, sem_inv_chain, sums_inverted)


def sum_rows(t, half):
    return t["att_dram"].rearrange("n (j r) s -> (n j) r s", r=VW)[half * P:(half + 1) * P, HD, :]


def invert_sums(dve, t, sums, chain_sem, done):
    chain, parts = Chain(dve, chain_sem), t["inv_parts"]
    chain(dve.reciprocal(sums[:, :], sums[:, :]))
    for k in range(PARTS - 1):
        chain(dve.tensor_copy(parts[:, k, :], sums[:, :]))
        chain(dve.tensor_tensor(sums[:, :], sums[:, :], parts[:, k, :], ALU.subtract))
    dve.tensor_copy(parts[:, PARTS - 1, :], sums[:, :]).then_inc(done, 1)


def load_block(eng, t, blk, u):
    sums_at = t["att_dram"].rearrange("n (j r) s -> n j r s", j=BPS)
    inverses = t["inverse_dram"].rearrange("(n j) k s -> n j k s", j=BPS)
    j = ds(blk % BPS, 1)
    for c in range(KC):
        heads = ds((blk // BPS) * H + c * (H // KC), H // KC)
        eng.dma_start(t["num_ring"][u][:, c, :], sums_at[heads, j, 0:HD, :].rearrange("n j r s -> (n j) r s")).then_inc(t["out_loaded"][u], 16)
    eng.dma_start(t["inv_ring"][u][:, :], inverses[ds((blk // BPS) * H, H), j].rearrange("n j k s -> (n j) k s")).then_inc(t["out_loaded"][u], 16)


def output(nc, sem, sb, ps, t):
    AHEAD = 2
    wo_hi, wo_lo = sb("wo_hi", [P, KC, D], F32R), sb("wo_lo", [P, KC, D], F32R)
    num_hi = [sb(f"num_hi{u}", [P, KC, BLK], F32R) for u in range(RING)]
    num_lo = [sb(f"num_lo{u}", [P, KC, BLK], F32R) for u in range(RING)]
    wo_rounded, wo_split = sem("o_wo_rounded"), sem("o_wo_split")
    rounded, split = sem("o_rounded"), sem("o_split")
    num, inv, loaded = t["num_ring"], t["inv_ring"], t["out_loaded"]
    LOADS = KC + 1
    first = lambda u: 16 if u == 0 else 0
    sums = sb("sums2", [P, BLK])
    sums_in, sums_inverted, inv_chain = sem("o_sums_in"), sem("o_sums_inverted"), sem("o_inv_chain")
    res = [sb(f"res{u}", [P, TPB, D]) for u in range(2)]
    y_ps = [ps(f"y_ps{j}", [P, 2, D]) for j in range(4)]
    inv_ps = [ps(f"inv_ps{u}", [P, KC, BLK]) for u in range(2)]
    stored = [sem(f"o_stored{u}") for u in range(2)]
    spread_out = sem("o_spread")
    divided = sem("o_divided")
    projected = sem("o_projected")
    added = sem("o_added")

    with nc.Block() as block:
        @block.sync
        def _(sp):
            sp.dma_start(sums[:, :], sum_rows(t, 1)).then_inc(sums_in, 16)
            for blk in range(1, RING):
                load_block(sp, t, blk, blk)
            sp.wait_ge(sums_inverted, 1)
            sp.dma_start(t["inverse_dram"][P:2 * P], t["inv_parts"][:, :, :]).then_inc(sums_in, 16)

            def reload(i):
                for u in range(RING):
                    sp.wait_ge(split, (i - 1) * RING + u + 1)
                    load_block(sp, t, i * RING + u, u)

            assert NBLK // 2 % RING == 0
            with sp.Fori(1, NBLK // 2 // RING) as i:
                reload(i)
            sp.wait_ge(sums_in, 32)
            with sp.Fori(NBLK // 2 // RING, NBLK // RING) as i:
                reload(i)

        @block.vector
        def _(dve):
            dve.sem_inc(added, 4)
            dve.sem_inc(divided, 2)

            def divide(i, u):
                dve.wait_ge(spread_out, i * RING + u + 1)
                dve.tensor_tensor(num[u][:, :, :], num[u][:, :, :], inv_ps[u % 2][:, :, :], ALU.mult).then_inc(divided, 1)

            def add(i, u):
                blk = i * RING + u
                dve.wait_ge(stored[u % 2], (i * (RING // 2) + u // 2 + 1) * 16)
                for j in range(2):
                    dve.wait_ge(projected, blk * 2 + j + 1 + 2 * RING)
                    dve.tensor_tensor(res[u % 2][:, 2 * j:2 * j + 2, :], y_ps[2 * (u % 2) + j][:, :, :],
                                      t["tok_all"][:, ds(blk, 1), 2 * j * D:(2 * j + 2) * D].rearrange("p n (k d) -> p (n k) d", k=2),
                                      ALU.add).then_inc(added, 1)

            for u in range(AHEAD):
                divide(0, u)
            dve.wait_ge(sums_in, 16)
            invert_sums(dve, t, sums, inv_chain, sums_inverted)
            with dve.Fori(0, NBLK // RING - 1) as i:
                for u in range(RING):
                    divide(i + (u + AHEAD) // RING, (u + AHEAD) % RING)
                    add(i, u)
            i = NBLK // RING - 1
            for u in range(RING):
                if u + AHEAD < RING:
                    divide(i, u + AHEAD)
                add(i, u)

        @block.tensor
        def _(pe):
            def hand_out(i, u):
                pe.wait_ge(loaded[u], (i + 1) * 16 * LOADS + first(u))
                pe.wait_ge(divided, i * RING + u + 1)
                for c in range(KC):
                    ins = pe.matmul(inv_ps[u % 2][:, c, :], t["spread"][:, c * P:(c + 1) * P], inv[u][:, :], start=True, stop=True)
                ins.then_inc(spread_out, 1)

            def project(i, u):
                blk = i * RING + u
                pe.wait_ge(split, blk + 1)
                for j in range(2):
                    pe.wait_ge(added, blk * 2 + j + 1)
                    for k in range(2):
                        tok = (2 * j + k) * P
                        for c in range(KC):
                            hi, lo = (part[u][:, c, tok:tok + P] for part in (num_hi, num_lo))
                            for m, (v, w) in enumerate(((hi, wo_hi), (hi, wo_lo), (lo, wo_hi))):
                                ins = pe.matmul(y_ps[2 * (u % 2) + j][:, k, :], v, w[:, c, :],
                                                start=(c == 0 and m == 0), stop=(c == KC - 1 and m == 2))
                    ins.then_inc(projected, 1)

            pe.sem_inc(projected, 2 * RING)
            for u in range(AHEAD):
                hand_out(0, u)
            pe.wait_ge(wo_split, 1)
            with pe.Fori(0, NBLK // RING - 1) as i:
                for u in range(RING):
                    hand_out(i + (u + AHEAD) // RING, (u + AHEAD) % RING)
                    project(i, u)
            i = NBLK // RING - 1
            for u in range(RING):
                if u + AHEAD < RING:
                    hand_out(i, u + AHEAD)
                project(i, u)

        @block.gpsimd
        def _(pool):
            pool.wait_ge(wo_rounded, 1)
            pool.tensor_tensor(wo_lo[:, :, :], t["woT_sb"][:, :, :], wo_hi[:, :, :].bitcast(F32), ALU.subtract).then_inc(wo_split, 1)
            with pool.Fori(0, NBLK // RING) as i:
                for u in range(RING):
                    pool.wait_ge(rounded, i * RING + u + 1)
                    pool.tensor_tensor(num_lo[u][:, :, :], num[u][:, :, :], num_hi[u][:, :, :].bitcast(F32), ALU.subtract).then_inc(split, 1)

        @block.scalar
        def _(act):
            for u in range(2):
                act.sem_inc(stored[u], 16)
            act.wait_ge(loaded[0], 16 * (LOADS + 1))
            act.activation(wo_hi[:, :, :], t["woT_sb"][:, :, :], ACT.Copy).then_inc(wo_rounded, 1)

            def round_quotients(i, u):
                act.wait_ge(projected, (i * RING + u) * 2 + 2)
                act.wait_ge(divided, i * RING + u + 3)
                act.activation(num_hi[u][:, :, :], num[u][:, :, :], ACT.Copy).then_inc(rounded, 1)

            def store(i, u):
                blk = i * RING + u
                act.wait_ge(added, blk * 2 + 6)
                act.dma_start(t["out_blocks"][ds(blk, 1)].rearrange("n p t d -> (n p) t d"), res[u % 2][:, :, :]).then_inc(stored[u % 2], 16)

            for u in range(AHEAD):
                round_quotients(0, u)
            with act.Fori(0, NBLK // RING - 1) as i:
                for u in range(RING):
                    round_quotients(i + (u + AHEAD) // RING, (u + AHEAD) % RING)
                    store(i, u)
            i = NBLK // RING - 1
            for u in range(RING):
                if u + AHEAD < RING:
                    round_quotients(i, u + AHEAD)
                store(i, u)
            for u in range(2):
                act.wait_ge(stored[u], 16 * (NBLK // 2 + 1))


def kernel(**inputs):
    import numpy as np
    import concourse.bacc as bacc
    from concourse.bass_utils import run_bass_kernel_spmd

    get = {k: np.asarray(v) for k, v in inputs.items()}
    a = {
        "x": get["L0_attn_hidden_states"].reshape(TOKENS, D),
        **{w + "T": get[f"L0_attn_{n}"].T for w, n in (("wq", "Wq"), ("wk", "Wk"), ("wv", "Wv"), ("wo", "Wo"))},
        "bq": get["L0_attn_bq"].reshape(KC, P).T,
        "bk": get["L0_attn_bk"].reshape(KC, P).T,
        "bv": get["L0_attn_bv"], "bo": get["L0_attn_bo"],
        "wg": get["L0_ffn_wg"], "bg": get["L0_ffn_bg"],
        "w1": get["L0_ffn_w1"].transpose(1, 0, 2).reshape(D, E * F),
        "b1": get["L0_ffn_b1"].reshape(EP, P).T,
        "w2": get["L0_ffn_w2"].reshape(E * F, D), "b2": get["L0_ffn_b2"],
        "gamma": get["L0_ffn_gamma"], "beta": get["L0_ffn_beta"],
    }
    a = {k: np.ascontiguousarray(v) for k, v in a.items()}
    nc = bacc.Bacc("TRN2", target_bir_lowering=False, num_devices=1)
    args = {k: nc.dram_tensor(f"in_{k}", v.shape, F32, kind="ExternalInput").ap() for k, v in a.items()}
    args["out"] = nc.dram_tensor("out", (TOKENS, D), F32, kind="ExternalOutput").ap()
    build(nc, **args)
    r = run_bass_kernel_spmd(nc, [{f"in_{k}": v for k, v in a.items()}], core_ids=[0])
    return r.results[0]["out"].reshape(B, S, D)
```
